# Optimizing a Trainium2 kernel written in Bass

```python
import numpy as np
import jax
import jax.numpy as jnp

def _softmax(x, axis=-1):
    return jax.nn.softmax(x, axis=axis)

def _gelu(x):
    return jax.nn.gelu(x, approximate=True)

def _silu(x):
    return jax.nn.silu(x)

def _sigmoid(x):
    return jax.nn.sigmoid(x)

def _layernorm(x, axis=-1, eps=1e-05):
    m = jnp.mean(x, axis=axis, keepdims=True)
    v = jnp.var(x, axis=axis, keepdims=True)
    return (x - m) / jnp.sqrt(v + eps)

def _scatter_add(tgt, idx, src, axis=0):
    return tgt.at[idx].add(src)

def _segment_sum(src, seg, n):
    return jax.ops.segment_sum(src, seg, n)
kernel_name = 'mk_prb_d1_jaxref_r8_a768bb'

def setup_inputs(seed: int=0):
    np.random.seed(seed)
    _w = jnp.asarray

    def _L0_attn_setup():
        import jax, jax.numpy as jnp
        import numpy as np
        B, T, C, FFN, N_LAYER, LAYER_ID = (4, 256, 128, 512, 24, 1)
        EPS = 1e-05

        def _ln(z, g, b):
            m = jnp.mean(z, axis=-1, keepdims=True)
            v = jnp.mean(jnp.square(z - m), axis=-1, keepdims=True)
            return (z - m) * jax.lax.rsqrt(v + EPS) * g + b

        def _shift(z):
            return jnp.pad(z, ((0, 0), (1, 0), (0, 0)))[:, :-1]

        def _wkv(time_decay, u, k, v):
            w = -jnp.exp(time_decay)
            kt = jnp.moveaxis(k, 1, 0)
            vt = jnp.moveaxis(v, 1, 0)
            aa = jnp.zeros_like(kt[0])
            bb = jnp.zeros_like(kt[0])
            pp = jnp.full_like(kt[0], -1e+38)

            def step(carry, kv):
                aa, bb, pp = carry
                kk, vv = kv
                ww = u + kk
                p = jnp.maximum(pp, ww)
                e1 = jnp.exp(pp - p)
                e2 = jnp.exp(ww - p)
                out = (e1 * aa + e2 * vv) / (e1 * bb + e2)
                ww2 = pp + w
                p2 = jnp.maximum(ww2, kk)
                e1b = jnp.exp(ww2 - p2)
                e2b = jnp.exp(kk - p2)
                return ((e1b * aa + e2b * vv, e1b * bb + e2b, p2), out)
            _, out = jax.lax.scan(step, (aa, bb, pp), (kt, vt))
            return jnp.moveaxis(out, 0, 1)
        key = jax.random.key(seed)
        ks = jax.random.split(key, 10)
        scale = 0.02

        def w(k, shape):
            return jax.random.normal(k, shape, jnp.float32) * scale
        r01 = LAYER_ID / (N_LAYER - 1)
        r10 = 1.0 - LAYER_ID / N_LAYER
        ddd = np.arange(C, dtype=np.float64) / C
        h = np.arange(C, dtype=np.float64)
        decay = -5.0 + 8.0 * (h / (C - 1)) ** (0.7 + 1.3 * r01)
        zigzag = np.array([(i + 1) % 3 - 1 for i in range(C)], dtype=np.float64) * 0.5
        tfirst = np.log(0.3) + zigzag
        return {'x': jax.random.normal(ks[0], (B, T, C), jnp.float32), 'ln1_w': jnp.ones((C,), jnp.float32), 'ln1_b': jnp.zeros((C,), jnp.float32), 'ln2_w': jnp.ones((C,), jnp.float32), 'ln2_b': jnp.zeros((C,), jnp.float32), 'time_decay': jnp.asarray(decay, jnp.float32), 'time_first': jnp.asarray(tfirst, jnp.float32), 'tmk': jnp.asarray(ddd ** r10, jnp.float32), 'tmv': jnp.asarray(ddd ** r10 + 0.3 * r01, jnp.float32), 'tmr': jnp.asarray(ddd ** (0.5 * r10), jnp.float32), 'att_kw': w(ks[1], (C, C)), 'att_vw': w(ks[2], (C, C)), 'att_rw': w(ks[3], (C, C)), 'att_ow': w(ks[4], (C, C)), 'f_tmk': jnp.asarray(ddd ** r10, jnp.float32), 'f_tmr': jnp.asarray(ddd ** r10, jnp.float32), 'f_kw': w(ks[5], (FFN, C)), 'f_rw': w(ks[6], (C, C)), 'f_vw': w(ks[7], (C, FFN))}
    _L0_attn_in = _L0_attn_setup()

    def _L0_ffn_setup():
        import jax, jax.numpy as jnp
        import numpy as np
        B, S, H, M, E, K = (4, 256, 128, 512, 8, 2)
        key = jax.random.key(seed)
        ks = jax.random.split(key, 6)
        x = jax.random.normal(ks[0], (B, S, H), dtype=jnp.float32)
        Wr = jax.random.normal(ks[1], (E, H), dtype=jnp.float32) * (1.0 / np.sqrt(H))
        W1 = jax.random.normal(ks[2], (E, M, H), dtype=jnp.float32) * np.sqrt(2.0 / (H + M))
        b1 = jax.random.normal(ks[3], (E, M), dtype=jnp.float32) * 1e-06
        W2 = jax.random.normal(ks[4], (E, H, M), dtype=jnp.float32) * np.sqrt(2.0 / (H + M))
        b2 = jax.random.normal(ks[5], (E, H), dtype=jnp.float32) * 1e-06
        return {'x': x, 'Wr': Wr, 'W1': W1, 'b1': b1, 'W2': W2, 'b2': b2}
    _L0_ffn_in = _L0_ffn_setup()
    _d = {'L0_attn_x': _L0_attn_in['x'], 'L0_attn_ln1_w': _L0_attn_in['ln1_w'], 'L0_attn_ln1_b': _L0_attn_in['ln1_b'], 'L0_attn_ln2_w': _L0_attn_in['ln2_w'], 'L0_attn_ln2_b': _L0_attn_in['ln2_b'], 'L0_attn_time_decay': _L0_attn_in['time_decay'], 'L0_attn_time_first': _L0_attn_in['time_first'], 'L0_attn_tmk': _L0_attn_in['tmk'], 'L0_attn_tmv': _L0_attn_in['tmv'], 'L0_attn_tmr': _L0_attn_in['tmr'], 'L0_attn_att_kw': _L0_attn_in['att_kw'], 'L0_attn_att_vw': _L0_attn_in['att_vw'], 'L0_attn_att_rw': _L0_attn_in['att_rw'], 'L0_attn_att_ow': _L0_attn_in['att_ow'], 'L0_attn_f_tmk': _L0_attn_in['f_tmk'], 'L0_attn_f_tmr': _L0_attn_in['f_tmr'], 'L0_attn_f_kw': _L0_attn_in['f_kw'], 'L0_attn_f_rw': _L0_attn_in['f_rw'], 'L0_attn_f_vw': _L0_attn_in['f_vw'], 'L0_ffn_Wr': _L0_ffn_in['Wr'], 'L0_ffn_W1': _L0_ffn_in['W1'], 'L0_ffn_b1': _L0_ffn_in['b1'], 'L0_ffn_W2': _L0_ffn_in['W2'], 'L0_ffn_b2': _L0_ffn_in['b2']}
    _x0 = _d['L0_attn_x']
    _d['L0_attn_x'] = jax.random.normal(jax.random.fold_in(jax.random.key(seed), 1), (4, 1024, 128), dtype=_x0.dtype)
    del _x0
    return _d

def reference(L0_attn_x, L0_attn_ln1_w, L0_attn_ln1_b, L0_attn_ln2_w, L0_attn_ln2_b, L0_attn_time_decay, L0_attn_time_first, L0_attn_tmk, L0_attn_tmv, L0_attn_tmr, L0_attn_att_kw, L0_attn_att_vw, L0_attn_att_rw, L0_attn_att_ow, L0_attn_f_tmk, L0_attn_f_tmr, L0_attn_f_kw, L0_attn_f_rw, L0_attn_f_vw, L0_ffn_Wr, L0_ffn_W1, L0_ffn_b1, L0_ffn_W2, L0_ffn_b2):

    def _L0_attn_ref(x, ln1_w, ln1_b, ln2_w, ln2_b, time_decay, time_first, tmk, tmv, tmr, att_kw, att_vw, att_rw, att_ow, f_tmk, f_tmr, f_kw, f_rw, f_vw):
        import jax, jax.numpy as jnp
        import numpy as np
        B, T, C, FFN, N_LAYER, LAYER_ID = (4, 256, 128, 512, 24, 1)
        EPS = 1e-05

        def _ln(z, g, b):
            m = jnp.mean(z, axis=-1, keepdims=True)
            v = jnp.mean(jnp.square(z - m), axis=-1, keepdims=True)
            return (z - m) * jax.lax.rsqrt(v + EPS) * g + b

        def _shift(z):
            return jnp.pad(z, ((0, 0), (1, 0), (0, 0)))[:, :-1]

        def _wkv(time_decay, u, k, v):
            w = -jnp.exp(time_decay)
            kt = jnp.moveaxis(k, 1, 0)
            vt = jnp.moveaxis(v, 1, 0)
            aa = jnp.zeros_like(kt[0])
            bb = jnp.zeros_like(kt[0])
            pp = jnp.full_like(kt[0], -1e+38)

            def step(carry, kv):
                aa, bb, pp = carry
                kk, vv = kv
                ww = u + kk
                p = jnp.maximum(pp, ww)
                e1 = jnp.exp(pp - p)
                e2 = jnp.exp(ww - p)
                out = (e1 * aa + e2 * vv) / (e1 * bb + e2)
                ww2 = pp + w
                p2 = jnp.maximum(ww2, kk)
                e1b = jnp.exp(ww2 - p2)
                e2b = jnp.exp(kk - p2)
                return ((e1b * aa + e2b * vv, e1b * bb + e2b, p2), out)
            _, out = jax.lax.scan(step, (aa, bb, pp), (kt, vt))
            return jnp.moveaxis(out, 0, 1)
        h = _ln(x, ln1_w, ln1_b)
        hx = _shift(h)
        xk = h * tmk + hx * (1.0 - tmk)
        xv = h * tmv + hx * (1.0 - tmv)
        xr = h * tmr + hx * (1.0 - tmr)
        k = jnp.einsum('btc,dc->btd', xk, att_kw)
        v = jnp.einsum('btc,dc->btd', xv, att_vw)
        sr = jax.nn.sigmoid(jnp.einsum('btc,dc->btd', xr, att_rw))
        rwkv = sr * _wkv(time_decay, time_first, k, v)
        x = x + jnp.einsum('btd,cd->btc', rwkv, att_ow)
        h = _ln(x, ln2_w, ln2_b)
        hx = _shift(h)
        xk = h * f_tmk + hx * (1.0 - f_tmk)
        xr = h * f_tmr + hx * (1.0 - f_tmr)
        kk = jnp.square(jax.nn.relu(jnp.einsum('btc,fc->btf', xk, f_kw)))
        kv = jnp.einsum('btf,cf->btc', kk, f_vw)
        x = x + jax.nn.sigmoid(jnp.einsum('btc,dc->btd', xr, f_rw)) * kv
        return x

    def _L0_ffn_ref(x, Wr, W1, b1, W2, b2):
        import jax, jax.numpy as jnp
        import numpy as np
        B, S, H, M, E, K = (4, 256, 128, 512, 8, 2)
        logits = jnp.einsum('bsh,eh->bse', x, Wr)
        probs = jax.nn.softmax(logits, axis=-1)
        top_v, top_i = jax.lax.top_k(probs, K)
        top_v = top_v / jnp.sum(top_v, axis=-1, keepdims=True)
        out = jnp.zeros_like(x)
        for e in range(E):
            w_e = jnp.sum(jnp.where(top_i == e, top_v, 0.0), axis=-1)
            h = jnp.einsum('bsh,mh->bsm', x, W1[e]) + b1[e]
            h = jax.nn.gelu(h, approximate=False)
            y = jnp.einsum('bsm,hm->bsh', h, W2[e]) + b2[e]
            out = out + y * w_e[..., None]
        return out
    x = L0_attn_x
    xn = _layernorm(x, axis=-1)
    x = x + _L0_attn_ref(xn, L0_attn_ln1_w, L0_attn_ln1_b, L0_attn_ln2_w, L0_attn_ln2_b, L0_attn_time_decay, L0_attn_time_first, L0_attn_tmk, L0_attn_tmv, L0_attn_tmr, L0_attn_att_kw, L0_attn_att_vw, L0_attn_att_rw, L0_attn_att_ow, L0_attn_f_tmk, L0_attn_f_tmr, L0_attn_f_kw, L0_attn_f_rw, L0_attn_f_vw) + _L0_ffn_ref(xn, L0_ffn_Wr, L0_ffn_W1, L0_ffn_b1, L0_ffn_W2, L0_ffn_b2)
    return x

_drawn_inputs = setup_inputs


def setup_inputs(seed=0):
    import zlib

    import numpy as np

    out = dict(_drawn_inputs(seed))
    spreads = {'L0_attn_ln1_w': (1.0, 0.6),
     'L0_attn_ln1_b': (0.0, 0.8),
     'L0_attn_ln2_w': (1.0, 0.6),
     'L0_attn_ln2_b': (0.0, 0.8)}
    factors = {'L0_attn_time_decay': 8.0,
     'L0_attn_time_first': 8.0,
     'L0_attn_tmk': 8.0,
     'L0_attn_tmv': 8.0,
     'L0_attn_tmr': 8.0,
     'L0_attn_att_kw': 8.0,
     'L0_attn_att_vw': 8.0,
     'L0_attn_att_rw': 8.0,
     'L0_attn_att_ow': 8.0,
     'L0_attn_f_tmk': 8.0,
     'L0_attn_f_tmr': 8.0,
     'L0_attn_f_kw': 8.0,
     'L0_attn_f_rw': 8.0,
     'L0_attn_f_vw': 8.0,
     'L0_ffn_b1': 64.0,
     'L0_ffn_b2': 64.0,
     'L0_ffn_Wr': 8.0,
     'L0_ffn_W1': 8.0,
     'L0_ffn_W2': 8.0}
    for name, (base, spread) in spreads.items():
        noise = np.random.default_rng([zlib.crc32(name.encode()), seed]).standard_normal(out[name].shape)
        drawn = base * np.exp(spread * noise) if base else spread * noise
        out[name] = jnp.asarray(drawn.astype(out[name].dtype))
    for name, factor in factors.items():
        out[name] = (out[name] * factor).astype(out[name].dtype)
    return out
```

```python
import numpy as np
import concourse.bass as bass
from concourse import mybir
from contextlib import ExitStack

P = 128
BATCH, TIME, CH = 4, 1024, 128
TOK = 512
NT = TOK // P
CHUNKS = BATCH * TIME // TOK
PAIR = TIME // TOK
EXP = 8
HID = 512
HC = HID // P
EPS = 1e-5
NEG_BIG = -1e38
MASKED = -3e38

(LN1_W, LN1_B, LN2_W, LN2_B, DECAY, FIRST, TMK, TMV, TMR, F_TMK, F_TMR) = range(11)
VECTORS = 11
PROJ = ("k", "v", "r", "o", "fr")

EVENTS = dict(
    up_done=EXP * HC, y_done=EXP, k_ps=1, v_ps=1, r_ps=1, xnT_ps=1, zT_ps=1, logit_ps=1, wT_ps=1,
    o_ps=1, h2T_ps=1, fr_ps=1, fk_ps=HC, fv_ps=1, fin_ps=1,
    gelu_done=EXP * HC, k_sb=1, v_sb=1, h1_ready=1, exp_done=1, rt_ready=1, ed_ready=1, wT_sb=1,
    h2_ready=1, th_ready=1, relu_done=HC, kk_ready=HC,
    y_taken=EXP, xsplit=2, stat1=1, norm1=1, mix1=1, args_ready=1, logit_sb=1, ed_arg=1, w_ready=1,
    rw_ready=1, x1_ready=1, stat2=1, norm2=1, mix2=1, fin_ready=1, out_ready=1,
    moe_added=EXP - 1, rstd1=1, rstd2=1, n2_ready=1, xs_ready=1,
    x_loaded=16, w_stored=16, w_spread=16, out_stored=16,
)

AHEAD = dict(
    tensor=("fin_ps", "fk_ps", "fv_ps", "o_ps"), vector=("fin_ready", "mix2", "out_ready"),
    gpsimd=("moe_added",), sync=("out_stored",),
)


def build(nc, x, vec, projs, fk, fv, wr, w1, b1, w2, b2, out):
    f32, f32r = mybir.dt.float32, mybir.dt.float32r
    ALU, ACT, AX = mybir.AluOpType, mybir.ActivationFunctionType, mybir.AxisListType

    ctx = ExitStack()
    with ctx:
        def sb(name, shape, dt=f32):
            return ctx.enter_context(nc.sbuf_tensor(name, shape, dt))

        def sem(name):
            return ctx.enter_context(nc.semaphore(name))

        vec_sb = sb("vec_sb", [P, VECTORS])
        negw = sb("negw", [P, 1])
        proj_sb = sb("proj_sb", [P, len(PROJ), P])
        fk_sb = sb("fk_sb", [P, HID])
        fv_sb = sb("fv_sb", [P, HC, P])
        wr_sb = sb("wr_sb", [P, EXP])
        wr_hi, wr_lo = sb("wr_hi", [P, EXP], f32r), sb("wr_lo", [P, EXP], f32r)
        w1_hi, w1_lo = sb("w1_hi", [P, EXP, HID], f32r), sb("w1_lo", [P, EXP, HID], f32r)
        w2_sb = sb("w2_sb", [P, EXP, HC, P])
        b1_sb = sb("b1_sb", [P, EXP, HC])
        b2_sb = sb("b2_sb", [P, EXP])
        ident = sb("ident", [P, P])
        rank = sb("rank", [P, EXP])
        neg_half = sb("neg_half", [P, NT])

        x_tok = [sb(f"x_tok{i}", [P, NT, CH]) for i in range(2)]
        xn_tok = [sb(f"xn_tok{i}", [P, NT, CH]) for i in range(2)]
        z_tok = sb("z_tok", [P, NT, CH])
        x1_tok = sb("x1_tok", [P, NT, CH])
        z2_tok = z_tok
        xs_tok = sb("xs_tok", [P, NT, CH])
        out_sb = sb("out_sb", [P, NT, CH])
        bn1, bn2 = sb("bn1", [P, NT, 6]), sb("bn2", [P, NT, 6])
        mv1, mv2 = sb("mv1", [P, NT, 2]), sb("mv2", [P, NT, 2])
        ve1, ve2 = sb("ve1", [P, NT]), sb("ve2", [P, NT])
        ra, rb, rz = sb("ra", [P, NT]), sb("rb", [P, NT]), sb("rz", [P, NT])
        r2 = sb("r2", [P, NT])

        lg = sb("lg", [P, NT, EXP])
        lg2 = sb("lg2", [P, NT, EXP])
        eq, tie = sb("eq", [P, NT, EXP]), sb("tie", [P, NT, EXP])
        eq2, tie2 = sb("eq2", [P, NT, EXP]), sb("tie2", [P, NT, EXP])
        pick1, pick2 = sb("pick1", [P, NT, EXP]), sb("pick2", [P, NT, EXP])
        m1, m2 = sb("m1", [P, NT]), sb("m2", [P, NT])
        f1, f2 = sb("f1", [P, NT]), sb("f2", [P, NT])
        gap, ed = sb("gap", [P, NT]), sb("ed", [P, NT])
        dn, g1, g2 = sb("dn", [P, NT]), sb("g1", [P, NT]), sb("g2", [P, NT])
        wa, wb = sb("wa", [P, NT, EXP]), sb("wb", [P, NT, EXP])
        w_tok = sb("w_tok", [P, NT, EXP])
        wT = sb("wT", [EXP, TOK])
        w_bc = [sb(f"w_bc{i}", [P, EXP, TOK]) for i in range(2)]
        w1_raw = w_bc[1]

        x_hi = [sb(f"x_hi{i}", [P, TOK], f32r) for i in range(2)]
        x_lo = [sb(f"x_lo{i}", [P, TOK], f32r) for i in range(2)]
        h1 = [sb(f"h1_{i}", [P, 1 + TOK]) for i in range(2)]
        h2 = [sb(f"h2_{i}", [P, 1 + TOK]) for i in range(2)]
        dif = sb("dif", [P, TOK])
        xk, xv, xr = (sb(n, [P, TOK]) for n in ("xk", "xv", "xr"))
        xk2, xr2 = sb("xk2", [P, TOK]), sb("xr2", [P, TOK])
        kT, vT = sb("kT", [P, TOK]), sb("vT", [P, TOK])
        rt = kT
        pp = [sb(f"pp{i}", [P, 1 + TOK]) for i in range(2)]
        aa = [sb(f"aa{i}", [P, 1 + TOK]) for i in range(2)]
        bb = [sb(f"bb{i}", [P, 1 + TOK]) for i in range(2)]
        ex = sb("ex", [P, 4, TOK])
        E1B, E2B, E1, E2 = range(4)
        n2, num, den, rw = (sb(n, [P, TOK]) for n in ("n2", "num", "den", "rw"))
        e2v, pm = rw, num
        th = sb("th", [P, TOK])
        kk = sb("kk", [P, HC, TOK])
        g = sb("g", [P, 2, HC, TOK])
        y_w = sb("y_w", [P, 2, TOK])
        moe = sb("moe", [P, 2, TOK])
        gated, fin = dif, sb("fin", [P, TOK])

        def bank(name):
            return ctx.enter_context(nc.psum_tensor(name, [P, TOK], f32))

        H = [bank(f"ps_h{i}") for i in range(3)]
        Y = bank("ps_y")
        A = [bank(f"ps_a{i}") for i in range(4)]

        w_dram = nc.dram_tensor("w_scratch", [CHUNKS, EXP, TOK], f32, kind="Internal").ap()
        x_t = x.rearrange("(q n p) c -> q p n c", n=NT, p=P)
        out_t = out.rearrange("(q n p) c -> q p n c", n=NT, p=P)

        S = {name: sem(name) for name in EVENTS}
        x_in, vec_in, w1_in, late_in = sem("x_in"), sem("vec_in"), [sem(f"w1_in{e}") for e in range(EXP)], sem("late_in")
        const_ready, w1_split, dve_const, negw_ready = sem("const_ready"), sem("w1_split"), sem("dve_const"), sem("negw_ready")
        w1_hi_ready = sem("w1_hi_ready")
        dve_step, pool_step, act_step = sem("dve_step"), sem("pool_step"), sem("act_step")

        def until(eng, name, b, off, k):
            n = EVENTS[name]
            least = n * off + k
            ahead = n if any(name in names for names in AHEAD.values()) else 0
            if isinstance(b, int):
                if PAIR * n * b + least > 0:
                    eng.wait_ge(S[name], PAIR * n * b + least + ahead)
            else:
                assert least + ahead > 0, (name, off, k)
                eng.wait_ge(S[name], b * (PAIR * n) + (least + ahead))

        def signal_ahead(eng, which):
            for name in AHEAD[which]:
                eng.sem_inc(S[name], EVENTS[name])

        def steps(eng, own):
            count = [0]

            def step(ins):
                count[0] += 1
                ins.then_inc(own, 1)
                return count[0]

            def after(n):
                eng.wait_ge(own, n)

            def restart():
                if count[0]:
                    eng.wait_ge(own, count[0])
                    eng.sem_clear(own)
                    count[0] = 0
            return step, after, restart

        def schedule(eng, slot, restart=None):
            for e in range(2):
                slot(0, 0, e)
            if restart:
                restart()
            with eng.Fori(0, CHUNKS // PAIR - 1) as b:
                for off, es in ((0, range(2, EXP)), (1, range(EXP)), (2, range(2))):
                    for e in es:
                        slot(b, off, e)
                if restart:
                    restart()
            last = CHUNKS // PAIR - 1
            for off, es in ((0, range(2, EXP)), (1, range(EXP))):
                for e in es:
                    slot(last, off, e)

        def has(b, off):
            return not isinstance(b, int) or 0 <= PAIR * b + off < CHUNKS

        def bcast(t):
            return t[:].rearrange("p (n o) -> p n o", o=1).to_broadcast([P, NT, EXP])

        block = ctx.enter_context(nc.Block())

        @block.sync
        def _(sp):
            signal_ahead(sp, "sync")
            sp.dma_start(x_tok[0][:], x_t[0]).then_inc(S["x_loaded"], 16)
            sp.dma_start(vec_sb[:], vec).then_inc(vec_in, 16)
            sp.dma_start(wr_sb[:], wr).then_inc(vec_in, 16)
            sp.dma_start(b1_sb[:], b1).then_inc(vec_in, 16)
            sp.dma_start(b2_sb[:], b2).then_inc(vec_in, 16)
            for e in range(EXP):
                sp.dma_start(w1_raw[:, e, :], w1[:, e, :]).then_inc(w1_in[e], 16)
            def spread(q):
                until(sp, "wT_sb", 0, q, 1)
                sp.dma_start(w_dram[q], wT[:]).then_inc(S["w_stored"], 16)
                until(sp, "w_stored", 0, q, 16)
                until(sp, "y_taken", 0, q - 2, EXP)
                if q == 1:
                    sp.wait_ge(w1_split, EXP + 1)
                sp.dma_start(w_bc[q % 2][:], w_dram[q:q + 1].to_broadcast([P, EXP, TOK]))\
                  .then_inc(S["w_spread"], 16)

            def load(q):
                until(sp, "xs_ready", 0, q - 2, 1)
                until(sp, "x_loaded", 0, q - 1, 16)
                sp.dma_start(x_tok[q % 2][:], x_t[q]).then_inc(S["x_loaded"], 16)

            def store(q):
                until(sp, "out_ready", 0, q, 1)
                sp.dma_start(out_t[q], out_sb[:]).then_inc(S["out_stored"], 16)

            load(1)
            spread(0)
            for q in range(CHUNKS):
                if q > 0:
                    store(q - 1)
                if q + 1 < CHUNKS:
                    spread(q + 1)
                if q + 2 < CHUNKS:
                    load(q + 2)
            store(CHUNKS - 1)
            until(sp, "out_stored", 0, CHUNKS - 1, 16)

        @block.tensor
        def _(pe):
            def split_mm(dst, w_h, w_l, a_h, a_l):
                nc.tensor.matmul(dst, w_h, a_h, start=True, stop=False)
                nc.tensor.matmul(dst, w_h, a_l, start=False, stop=False)
                return nc.tensor.matmul(dst, w_l, a_h, start=False, stop=True)

            def up(b, off, e):
                for m in range(HC):
                    i = HC * e + m
                    if i == 0:
                        until(pe, "xsplit", b, off, 2)
                    if i >= 3:
                        until(pe, "gelu_done", b, off, i - 2)
                    else:
                        until(pe, "gelu_done", b, off - 1, (31, 32, 30)[i])
                    cols = slice(m * P, (m + 1) * P)
                    split_mm(H[i % 3][:], w1_hi[:, e, cols], w1_lo[:, e, cols], x_hi[off % 2][:],
                             x_lo[off % 2][:]).then_inc(S["up_done"], 1)

            def down(b, off, e):
                until(pe, "y_taken", b, off, e)
                for m in range(HC):
                    until(pe, "gelu_done", b, off, HC * e + m + 1)
                    last = nc.tensor.matmul(Y[:], w2_sb[:, e, m, :], g[:, e % 2, m, :],
                                            start=(m == 0), stop=(m == HC - 1))
                last.then_inc(S["y_done"], 1)

            def turn(dst, src, name):
                for n in range(NT):
                    last = nc.tensor.transpose(dst[:, n * P:(n + 1) * P], src(n), ident[:])
                last.then_inc(S[name], 1)

            def front(b, off):
                until(pe, "norm1", b, off, 1)
                until(pe, "fin_ready", b, off - 2, 1)
                turn(A[2], lambda n: xn_tok[off % 2][:, n, :], "xnT_ps")
                turn(A[3], lambda n: z_tok[:, n, :], "zT_ps")

            def router(b, off):
                until(pe, "xsplit", b, off, 2)
                for n in range(NT):
                    cols = slice(n * P, (n + 1) * P)
                    last = split_mm(A[1][:, n * EXP:(n + 1) * EXP], x_hi[off % 2][:, cols], x_lo[off % 2][:, cols],
                                    wr_hi[:], wr_lo[:])
                last.then_inc(S["logit_ps"], 1)

            def turn_w(b, off):
                until(pe, "w_ready", b, off, 1)
                for n in range(NT):
                    last = nc.tensor.transpose(A[1][0:EXP, n * P:(n + 1) * P], w_tok[:, n, :], ident[:])
                last.then_inc(S["wT_ps"], 1)

            def slot(b, off, e):
                if e + 1 < EXP:
                    up(b, off, e + 1)
                elif has(b, off + 1):
                    up(b, off + 1, 0)
                down(b, off, e)
                if e == 0:
                    until(pe, "mix1", b, off, 1)
                    until(pe, "th_ready", b, off - 1, 1)
                    nc.tensor.matmul(A[0][:], proj_sb[:, 0, :], xk[:], start=True, stop=True).then_inc(S["k_ps"], 1)
                    until(pe, "relu_done", b, off - 1, HC)
                    nc.tensor.matmul(A[1][:], proj_sb[:, 1, :], xv[:], start=True, stop=True).then_inc(S["v_ps"], 1)
                    if has(b, off + 1):
                        front(b, off + 1)
                if e == 1:
                    until(pe, "k_sb", b, off, 1)
                    nc.tensor.matmul(A[0][:], proj_sb[:, 2, :], xr[:], start=True, stop=True).then_inc(S["r_ps"], 1)
                    if has(b, off + 1):
                        until(pe, "v_sb", b, off, 1)
                        router(b, off + 1)
                        until(pe, "h1_ready", b, off + 1, 1)
                    if not (isinstance(b, int) and PAIR * b + off == 0):
                        until(pe, "fin_ready", b, off - 1, 1)
                        turn(A[3], lambda n: fin[:, n * P:(n + 1) * P], "fin_ps")
                if e == 3 and has(b, off + 1):
                    turn_w(b, off + 1)
                if e == 4:
                    until(pe, "rw_ready", b, off, 1)
                    if has(b, off + 1):
                        until(pe, "xsplit", b, off + 1, 2)
                    for n in range(NT):
                        last = nc.tensor.matmul(A[2][:, n * P:(n + 1) * P], rw[:, n * P:(n + 1) * P], proj_sb[:, 3, :],
                                                start=True, stop=True)
                    last.then_inc(S["o_ps"], 1)
                if e == 5:
                    until(pe, "norm2", b, off, 1)
                    until(pe, "out_ready", b, off - 1, 1)
                    turn(A[3], lambda n: z2_tok[:, n, :], "h2T_ps")
                if e == 6:
                    until(pe, "mix2", b, off, 1)
                    until(pe, "rt_ready", b, off, 1)
                    nc.tensor.matmul(A[0][:], proj_sb[:, 4, :], xr2[:], start=True, stop=True).then_inc(S["fr_ps"], 1)
                    for j in range(HC):
                        if j == 0 and has(b, off + 1):
                            until(pe, "wT_sb", b, off + 1, 1)
                        if j == 0 and not has(b, off + 1):
                            until(pe, "v_sb", b, off, 1)
                        if j == 1:
                            until(pe, "x1_ready", b, off, 1)
                        if j == 2:
                            until(pe, "h2_ready", b, off, 1)
                        if j == 3:
                            until(pe, "relu_done", b, off, 1)
                        nc.tensor.matmul(A[(1, 2, 3, 1)[j]][:], fk_sb[:, j * P:(j + 1) * P], xk2[:],
                                         start=True, stop=True).then_inc(S["fk_ps"], 1)
                if e == 7:
                    until(pe, "relu_done", b, off, 2)
                    for j in range(HC):
                        until(pe, "kk_ready", b, off, j + 1)
                        last = nc.tensor.matmul(A[2][:], fv_sb[:, j, :], kk[:, j, :], start=(j == 0), stop=(j == HC - 1))
                    last.then_inc(S["fv_ps"], 1)

            signal_ahead(pe, "tensor")
            pe.wait_ge(const_ready, 4)
            front(0, 0)
            pe.wait_ge(w1_split, 1)
            router(0, 0)
            turn_w(0, 0)
            pe.wait_ge(w1_split, EXP + 1)
            up(0, 0, 0)
            pe.wait_ge(late_in, 16 * 4)
            schedule(pe, slot)
            last = CHUNKS // PAIR - 1
            until(pe, "fin_ready", last, 1, 1)
            turn(A[3], lambda n: fin[:, n * P:(n + 1) * P], "fin_ps")

        @block.scalar
        def _(act):
            act.dma_start(proj_sb[:], projs).then_inc(late_in, 16)
            act.dma_start(fk_sb[:], fk).then_inc(late_in, 16)
            act.dma_start(fv_sb[:], fv).then_inc(late_in, 16)
            act.dma_start(w2_sb[:], w2).then_inc(late_in, 16)

            def gelu(b, off, e):
                for m in range(HC):
                    i = HC * e + m
                    until(act, "up_done", b, off, i + 1)
                    if m == 0:
                        until(act, "y_done", b, off, e - 1)
                    nc.scalar.activation(g[:, e % 2, m, :], H[i % 3][:], ACT.Gelu,
                                         bias=b1_sb[:, e, m:m + 1]).then_inc(S["gelu_done"], 1)

            def scaled(b, off, h, src, w_col, b_col, name, freed):
                until(act, freed, b, off - 1, 1)
                if off % 2 == 1:
                    until(act, name, b, off - 1, 1)
                    nc.scalar.activation(h[1][:, 0:1], h[0][:, TOK:TOK + 1], ACT.Copy)
                nc.scalar.activation(h[off % 2][:, 1:1 + TOK], src, ACT.Identity, bias=vec_sb[:, b_col:b_col + 1],
                                     scale=vec_sb[:, w_col:w_col + 1]).then_inc(S[name], 1)

            def front(b, off):
                until(act, "zT_ps", b, off, 1)
                scaled(b, off, h1, A[3][:], LN1_W, LN1_B, "h1_ready", "mix1")

            def exp_gap(b, off):
                until(act, "ed_arg", b, off, 1)
                nc.scalar.activation(ed[:], gap[:], ACT.Exp).then_inc(S["ed_ready"], 1)

            def take_w(b, off):
                until(act, "wT_ps", b, off, 1)
                until(act, "w_stored", b, off - 1, 16)
                nc.scalar.activation(wT[:], A[1][0:EXP, :], ACT.Copy).then_inc(S["wT_sb"], 1)

            def slot(b, off, e):
                if e + 1 < EXP:
                    gelu(b, off, e + 1)
                elif has(b, off + 1):
                    gelu(b, off + 1, 0)
                if e == 0:
                    until(act, "k_ps", b, off, 1)
                    until(act, "rw_ready", b, off - 1, 1)
                    nc.scalar.activation(kT[:], A[0][:], ACT.Copy).then_inc(S["k_sb"], 1)
                    until(act, "v_ps", b, off, 1)
                    nc.scalar.activation(vT[:], A[1][:], ACT.Copy).then_inc(S["v_sb"], 1)
                    if has(b, off + 1):
                        front(b, off + 1)
                if e == 2:
                    until(act, "args_ready", b, off, 1)
                    until(act, "r_ps", b, off, 1)
                    nc.scalar.activation(rt[:], A[0][:], ACT.Tanh, scale=0.5).then_inc(S["rt_ready"], 1)
                    nc.scalar.activation(ex[:], ex[:], ACT.Exp).then_inc(S["exp_done"], 1)
                    if has(b, off + 1):
                        exp_gap(b, off + 1)
                if e == 3 and has(b, off + 1):
                    take_w(b, off + 1)
                if e == 5:
                    until(act, "h2T_ps", b, off, 1)
                    scaled(b, off, h2, A[3][:], LN2_W, LN2_B, "h2_ready", "mix2")
                if e == 6:
                    until(act, "fr_ps", b, off, 1)
                    nc.scalar.activation(th[:], A[0][:], ACT.Tanh, scale=0.5).then_inc(S["th_ready"], 1)
                    until(act, "fv_ps", b, off - 1, 1)
                    for j in range(HC + 1):
                        if j < HC:
                            until(act, "fk_ps", b, off, j + 1)
                            nc.scalar.activation(kk[:, j, :], A[(1, 2, 3, 1)[j]][:], ACT.Relu)\
                              .then_inc(S["relu_done"], 1)
                        if j > 0:
                            until(act, "relu_done", b, off, j)
                            nc.scalar.activation(kk[:, j - 1, :], kk[:, j - 1, :], ACT.Square)\
                              .then_inc(S["kk_ready"], 1)

            act.wait_ge(vec_in, 16 * 4)
            nc.scalar.activation(negw[:], vec_sb[:, DECAY:DECAY + 1], ACT.Exp).then_inc(act_step, 1)
            act.wait_ge(act_step, 1)
            nc.scalar.activation(negw[:], negw[:], ACT.Copy, scale=-1.0).then_inc(negw_ready, 1)
            act.wait_ge(dve_const, 5)
            front(0, 0)
            exp_gap(0, 0)
            take_w(0, 0)
            gelu(0, 0, 0)
            schedule(act, slot)

        @block.vector
        def _(dve):
            V = nc.vector
            step, after, restart = steps(dve, dve_step)

            def stats(src, bn, mv, ve, name):
                for n in range(NT):
                    t = step(V.bn_stats(bn[:, n, :], src[:, n, :]))
                for n in range(NT):
                    after(t - NT + 1 + n)
                    u = step(V.bn_aggr(mv[:, n, :], bn[:, n, :]))
                after(u)
                V.tensor_scalar(ve[:].rearrange("p (n o) -> p n o", o=1), mv[:, :, 1:2], EPS, None, ALU.add)\
                 .then_inc(S[name], 1)

            def normalize(dst, src, mv, r):
                for n in range(NT):
                    last = V.tensor_scalar(dst[:, n, :], src[:, n, :], mv[:, n, 0:1], r[:, n:n + 1],
                                           ALU.subtract, ALU.mult)
                return last

            def front_stats(b, off):
                until(dve, "x_loaded", b, off, 16)
                stats(x_tok[off % 2], bn1, mv1, ve1, "stat1")

            def front_norm(b, off):
                until(dve, "rstd1", b, off, 1)
                until(dve, "h2T_ps", b, off - 2, 1)
                until(dve, "zT_ps", b, off - 1, 1)
                normalize(xn_tok[off % 2], x_tok[off % 2], mv1, ra)
                normalize(z_tok, x_tok[off % 2], mv1, rz).then_inc(S["norm1"], 1)

            def split_x(b, off):
                until(dve, "xnT_ps", b, off, 1)
                until(dve, "up_done", b, off - 2, EXP * HC)
                V.tensor_copy(x_hi[off % 2][:], A[2][:]).then_inc(S["xsplit"], 1)
                until(dve, "xsplit", b, off, 1)
                V.tensor_tensor(x_lo[off % 2][:], A[2][:], x_hi[off % 2][:].bitcast(f32), ALU.subtract)\
                 .then_inc(S["xsplit"], 1)

            def mixes(h, diff, outs, name):
                now, before = h[:, 1:1 + TOK], h[:, 0:TOK]
                after(step(V.tensor_tensor(diff[:], now, before, ALU.subtract)))
                for dst, mu in outs:
                    last = V.scalar_tensor_tensor(out=dst[:], in0=diff[:], scalar=vec_sb[:, mu:mu + 1], in1=before,
                                                  op0=ALU.mult, op1=ALU.add)
                last.then_inc(S[name], 1)

            def mix1(b, off):
                until(dve, "h1_ready", b, off, 1)
                until(dve, "r_ps", b, off - 1, 1)
                until(dve, "mix2", b, off - 1, 1)
                mixes(h1[off % 2], dif, ((xk, TMK), (xv, TMV), (xr, TMR)), "mix1")

            def first_best(src, peak, same, tie_, f, pick):
                after(step(V.tensor_reduce(out=peak[:], in_=src[:], op=ALU.max, axis=AX.X)))
                after(step(V.tensor_tensor(same[:], src[:], bcast(peak), ALU.is_equal)))
                after(step(V.tensor_tensor(tie_[:], same[:], rank[:].rearrange("p (o e) -> p o e", o=1)
                                           .to_broadcast([P, NT, EXP]), ALU.mult)))
                after(step(V.tensor_reduce(out=f[:], in_=tie_[:], op=ALU.max, axis=AX.X)))
                after(step(V.tensor_tensor(pick[:], tie_[:], bcast(f), ALU.is_equal)))

            def choose(b, off):
                until(dve, "logit_ps", b, off, 1)
                V.tensor_copy(lg[:].rearrange("p n e -> p (n e)"), A[1][:, 0:NT * EXP]).then_inc(S["logit_sb"], 1)
                until(dve, "logit_sb", b, off, 1)
                first_best(lg, m1, eq, tie, f1, pick1)
                after(step(V.scalar_tensor_tensor(out=lg2[:], in0=pick1[:], scalar=MASKED, in1=lg[:],
                                                  op0=ALU.mult, op1=ALU.add)))
                first_best(lg2, m2, eq2, tie2, f2, pick2)
                V.tensor_tensor(gap[:], m2[:], m1[:], ALU.subtract).then_inc(S["ed_arg"], 1)

            def weigh(b, off):
                until(dve, "ed_ready", b, off, 1)
                after(step(V.tensor_scalar(dn[:], ed[:], 1.0, None, ALU.add)))
                after(step(V.reciprocal(g1[:], dn[:])))
                t = step(V.tensor_tensor(g2[:], ed[:], g1[:], ALU.mult))
                u = step(V.tensor_tensor(wa[:], pick1[:], bcast(g1), ALU.mult))
                after(t)
                v = step(V.tensor_tensor(wb[:], pick2[:], bcast(g2), ALU.mult))
                after(v)
                until(dve, "wT_ps", b, off - 1, 1)
                V.tensor_tensor(w_tok[:], wa[:], wb[:], ALU.add).then_inc(S["w_ready"], 1)

            def state_args(b, off):
                i = off % 2
                before, now = pp[i][:, 0:TOK], pp[i][:, 1:1 + TOK]
                u = vec_sb[:, FIRST:FIRST + 1]
                until(dve, "k_sb", b, off, 1)
                if i:
                    step(V.tensor_copy(pp[1][:, 0:1], pp[0][:, TOK:TOK + 1]))
                    step(V.tensor_copy(aa[1][:, 0:1], aa[0][:, TOK:TOK + 1]))
                    after(step(V.tensor_copy(bb[1][:, 0:1], bb[0][:, TOK:TOK + 1])))
                s = step(V.tensor_tensor_scan(now, negw[:, 0:1].to_broadcast([P, TOK]), kT[:], pp[i][:, 0:1],
                                              ALU.add, ALU.max))
                after(s)
                m = step(V.scalar_tensor_tensor(out=pm[:], in0=kT[:], scalar=u, in1=before, op0=ALU.add, op1=ALU.max))
                V.scalar_tensor_tensor(out=ex[:, E1B, :], in0=before, scalar=negw[:, 0:1], in1=now,
                                       op0=ALU.add, op1=ALU.subtract)
                V.tensor_tensor(ex[:, E2B, :], kT[:], now, ALU.subtract)
                after(m)
                V.tensor_tensor(ex[:, E1, :], before, pm[:], ALU.subtract)
                V.scalar_tensor_tensor(out=ex[:, E2, :], in0=kT[:], scalar=u, in1=pm[:],
                                       op0=ALU.add, op1=ALU.subtract).then_inc(S["args_ready"], 1)

            sums_step = [0]

            def scan_sums(b, off):
                i = off % 2
                until(dve, "exp_done", b, off, 1)
                until(dve, "v_sb", b, off, 1)
                until(dve, "o_ps", b, off - 1, 1)
                t = step(V.tensor_tensor(e2v[:], ex[:, E2B, :], vT[:], ALU.mult))
                u = step(V.tensor_tensor_scan(bb[i][:, 1:1 + TOK], ex[:, E1B, :], ex[:, E2B, :], bb[i][:, 0:1],
                                              ALU.mult, ALU.add))
                after(t)
                v = step(V.tensor_tensor_scan(aa[i][:, 1:1 + TOK], ex[:, E1B, :], e2v[:], aa[i][:, 0:1],
                                              ALU.mult, ALU.add))
                after(u)
                w = step(V.tensor_tensor(den[:], ex[:, E1, :], bb[i][:, 0:TOK], ALU.mult))
                after(v)
                step(V.tensor_tensor(num[:], ex[:, E1, :], aa[i][:, 0:TOK], ALU.mult))
                after(w)
                sums_step[0] = step(V.tensor_tensor(den[:], den[:], ex[:, E2, :], ALU.add))

            def receptance(b, off):
                until(dve, "rt_ready", b, off, 1)
                until(dve, "n2_ready", b, off, 1)
                after(sums_step[0])
                after(step(V.tensor_tensor(num[:], num[:], n2[:], ALU.add)))
                t = step(V.scalar_tensor_tensor(out=num[:], in0=rt[:], scalar=1.0, in1=num[:],
                                                op0=ALU.add, op1=ALU.mult))
                after(step(V.reciprocal(den[:], den[:])))
                V.scalar_tensor_tensor(out=rw[:], in0=num[:], scalar=0.5, in1=den[:], op0=ALU.mult, op1=ALU.mult).then_inc(S["rw_ready"], 1)

            def take_y(b, off, e):
                if e == 0:
                    until(dve, "w_spread", b, off, 16)
                until(dve, "y_done", b, off, e + 1)
                if e == 2:
                    until(dve, "moe_added", b, off - 1, EXP - 1)
                if e >= 3:
                    until(dve, "moe_added", b, off, e - 2)
                dst = moe[:, off % 2, :] if e == 0 else y_w[:, e % 2, :]
                V.scalar_tensor_tensor(out=dst, in0=Y[:], scalar=b2_sb[:, e:e + 1], in1=w_bc[off % 2][:, e, :],
                                       op0=ALU.add, op1=ALU.mult).then_inc(S["y_taken"], 1)

            def finish_gate(b, off):
                until(dve, "fv_ps", b, off, 1)
                until(dve, "th_ready", b, off, 1)
                until(dve, *(("mix1", b, off + 1, 1) if has(b, off + 1) else ("mix2", b, off, 1)))
                after(step(V.scalar_tensor_tensor(out=gated[:], in0=th[:], scalar=1.0, in1=A[2][:],
                                                  op0=ALU.add, op1=ALU.mult)))
                until(dve, "moe_added", b, off, EXP - 1)
                until(dve, "fin_ps", b, off - 1, 1)
                V.scalar_tensor_tensor(out=fin[:], in0=gated[:], scalar=0.5, in1=moe[:, off % 2, :],
                                       op0=ALU.mult, op1=ALU.add).then_inc(S["fin_ready"], 1)

            def finish_out(b, off):
                until(dve, "fin_ps", b, off, 1)
                until(dve, "xs_ready", b, off, 1)
                until(dve, "out_stored", b, off - 1, 16)
                V.tensor_tensor(out_sb[:].rearrange("p n c -> p (n c)"), A[3][:],
                                xs_tok[:].rearrange("p n c -> p (n c)"), ALU.add).then_inc(S["out_ready"], 1)

            def slot(b, off, e):
                first = isinstance(b, int) and PAIR * b + off == 0
                if e == 0 and not first:
                    finish_gate(b, off - 1)
                if e == 1:
                    if has(b, off + 1):
                        split_x(b, off + 1)
                    state_args(b, off)
                if e == 2:
                    if has(b, off + 1):
                        choose(b, off + 1)
                if e == 3:
                    if has(b, off + 1):
                        weigh(b, off + 1)
                    scan_sums(b, off)
                if e == 4:
                    receptance(b, off)
                if e == 5:
                    until(dve, "o_ps", b, off, 1)
                    V.tensor_tensor(x1_tok[:].rearrange("p n c -> p (n c)"), A[2][:],
                                    xn_tok[off % 2][:].rearrange("p n c -> p (n c)"), ALU.add).then_inc(S["x1_ready"], 1)
                    until(dve, "x1_ready", b, off, 1)
                    stats(x1_tok, bn2, mv2, ve2, "stat2")
                    until(dve, "rstd2", b, off, 1)
                    if has(b, off + 1):
                        until(dve, "zT_ps", b, off + 1, 1)
                    normalize(z2_tok, x1_tok, mv2, r2).then_inc(S["norm2"], 1)
                if e == 6:
                    until(dve, "h2_ready", b, off, 1)
                    until(dve, "fk_ps", b, off - 1, HC)
                    until(dve, "fin_ready", b, off - 1, 1)
                    mixes(h2[off % 2], dif, ((xr2, F_TMR), (xk2, F_TMK)), "mix2")
                    if has(b, off + 1):
                        mix1(b, off + 1)
                if e == 7 and has(b, off + 2):
                    front_stats(b, off + 2)
                    front_norm(b, off + 2)
                take_y(b, off, e)
                if e == 1 and not first:
                    finish_out(b, off - 1)

            signal_ahead(dve, "vector")
            for t in (h1[0], h2[0], aa[0], bb[0]):
                V.memset(t[:, 0:1], 0.0).then_inc(dve_const, 1)
            V.memset(pp[0][:, 0:1], NEG_BIG).then_inc(dve_const, 1)
            dve.wait_ge(dve_const, 5)
            front_stats(0, 0)
            front_norm(0, 0)
            dve.wait_ge(w1_hi_ready, 1)
            V.tensor_tensor(wr_lo[:], wr_sb[:], wr_hi[:].bitcast(f32), ALU.subtract).then_inc(w1_split, 1)
            split_x(0, 0)
            choose(0, 0)
            weigh(0, 0)
            for e in range(EXP):
                dve.wait_ge(w1_hi_ready, e + 2)
                V.tensor_tensor(w1_lo[:, e, :], w1_raw[:, e, :], w1_hi[:, e, :].bitcast(f32), ALU.subtract)\
                 .then_inc(w1_split, 1)
            mix1(0, 0)
            front_stats(0, 1)
            front_norm(0, 1)
            dve.wait_ge(negw_ready, 1)
            schedule(dve, slot, restart)
            last = CHUNKS // PAIR - 1
            finish_gate(last, 1)
            finish_out(last, 1)

        @block.gpsimd
        def _(pool):
            G = nc.gpsimd
            step, after, restart = steps(pool, pool_step)

            def add_y(b, off, e):
                until(pool, "y_taken", b, off, e + 1)
                if e > 1:
                    until(pool, "moe_added", b, off, e - 1)
                G.tensor_tensor(moe[:, off % 2, :], moe[:, off % 2, :], y_w[:, e % 2, :], ALU.add)\
                 .then_inc(S["moe_added"], 1)

            def roots1(b, off):
                until(pool, "stat1", b, off, 1)
                until(pool, "norm1", b, off - 1, 1)
                var = mv1[:, :, 1:2].rearrange("p n o -> p (n o)")
                after(step(G.tensor_tensor(ra[:], ve1[:], neg_half[:], ALU.pow)))
                after(step(G.tensor_tensor(rb[:], ra[:], ra[:], ALU.mult)))
                after(step(G.tensor_tensor(rb[:], rb[:], var, ALU.mult)))
                after(step(G.tensor_scalar(rb[:], rb[:], EPS, None, ALU.add)))
                after(step(G.tensor_tensor(rb[:], rb[:], neg_half[:], ALU.pow)))
                G.tensor_tensor(rz[:], ra[:], rb[:], ALU.mult).then_inc(S["rstd1"], 1)

            def slot(b, off, e):
                if e >= 2:
                    add_y(b, off, e - 1)
                elif e == 0 and not (isinstance(b, int) and PAIR * b + off == 0):
                    add_y(b, off - 1, EXP - 1)
                if e == 3:
                    until(pool, "exp_done", b, off, 1)
                    until(pool, "v_sb", b, off, 1)
                    G.tensor_tensor(n2[:], ex[:, E2, :], vT[:], ALU.mult).then_inc(S["n2_ready"], 1)
                if e == 5:
                    until(pool, "stat2", b, off, 1)
                    G.tensor_tensor(r2[:], ve2[:], neg_half[:], ALU.pow).then_inc(S["rstd2"], 1)
                    until(pool, "out_ready", b, off - 1, 1)
                    G.tensor_tensor(xs_tok[:], x_tok[off % 2][:], x1_tok[:], ALU.add).then_inc(S["xs_ready"], 1)
                if e == 7 and has(b, off + 2):
                    roots1(b, off + 2)

            signal_ahead(pool, "gpsimd")
            t = step(G.memset(neg_half[:], -0.5))
            step(G.memset(ident[:], 0.0))
            after(step(G.memset(rank[:], 0.0)))
            G.affine_select(out=ident[:], in_=ident[:], compare_op=ALU.not_equal, fill=1.0, base=0,
                            pattern=[[-1, P]], channel_multiplier=1).then_inc(const_ready, 1)
            for e in range(EXP):
                last = G.memset(rank[:, e:e + 1], float(EXP - e))
            last.then_inc(const_ready, 1)
            pool.wait_ge(const_ready, 2)
            roots1(0, 0)
            pool.wait_ge(vec_in, 16 * 4)
            G.tensor_scalar(wr_hi[:], wr_sb[:], 1.0, None, ALU.mult).then_inc(w1_hi_ready, 1)
            pool.sem_inc(const_ready, 2)
            for e in range(EXP):
                pool.wait_ge(w1_in[e], 16)
                G.tensor_scalar(w1_hi[:, e, :], w1_raw[:, e, :], 1.0, None, ALU.mult).then_inc(w1_hi_ready, 1)
            roots1(0, 1)
            schedule(pool, slot, restart)
            add_y(CHUNKS // PAIR - 1, 1, EXP - 1)


def kernel(L0_attn_x, L0_attn_ln1_w, L0_attn_ln1_b, L0_attn_ln2_w, L0_attn_ln2_b, L0_attn_time_decay,
           L0_attn_time_first, L0_attn_tmk, L0_attn_tmv, L0_attn_tmr, L0_attn_att_kw, L0_attn_att_vw,
           L0_attn_att_rw, L0_attn_att_ow, L0_attn_f_tmk, L0_attn_f_tmr, L0_attn_f_kw, L0_attn_f_rw,
           L0_attn_f_vw, L0_ffn_Wr, L0_ffn_W1, L0_ffn_b1, L0_ffn_W2, L0_ffn_b2):
    import concourse.bacc as bacc
    from concourse.bass_utils import run_bass_kernel_spmd

    def lay(a):
        return np.ascontiguousarray(a)

    a = np.asarray
    arrays = dict(
        x=lay(a(L0_attn_x).reshape(BATCH * TIME, CH)),
        vec=lay(np.stack([a(v) for v in (
            L0_attn_ln1_w, L0_attn_ln1_b, L0_attn_ln2_w, L0_attn_ln2_b, L0_attn_time_decay, L0_attn_time_first,
            L0_attn_tmk, L0_attn_tmv, L0_attn_tmr, L0_attn_f_tmk, L0_attn_f_tmr)], axis=1)),
        projs=lay(np.stack([a(w).T for w in (
            L0_attn_att_kw, L0_attn_att_vw, L0_attn_att_rw, L0_attn_att_ow, L0_attn_f_rw)], axis=1)),
        fk=lay(a(L0_attn_f_kw).T),
        fv=lay(a(L0_attn_f_vw).T.reshape(HC, P, CH).transpose(1, 0, 2)),
        wr=lay(a(L0_ffn_Wr).T),
        w1=lay(a(L0_ffn_W1).transpose(2, 0, 1)),
        b1=lay(a(L0_ffn_b1).reshape(EXP, HC, P).transpose(2, 0, 1)),
        w2=lay(a(L0_ffn_W2).transpose(0, 2, 1).reshape(EXP, HC, P, CH).transpose(2, 0, 1, 3)),
        b2=lay(a(L0_ffn_b2).T),
    )
    nc = bacc.Bacc("TRN2", target_bir_lowering=False, num_devices=1)
    args = [nc.dram_tensor(n, v.shape, mybir.dt.from_np(v.dtype), kind="ExternalInput").ap() for n, v in arrays.items()]
    out = nc.dram_tensor("out", (BATCH * TIME, CH), mybir.dt.float32, kind="ExternalOutput").ap()
    build(nc, *args, out)
    r = run_bass_kernel_spmd(nc, [arrays], core_ids=[0])
    return r.results[0]["out"].reshape(BATCH, TIME, CH)
```

```python
import numpy as np
import concourse.bass as bass
from concourse import mybir
from contextlib import ExitStack

P = 128
BATCH, TIME, CH = 4, 1024, 128
TOK = 512
NT = TOK // P
CHUNKS = BATCH * TIME // TOK
PAIR = TIME // TOK
EXP = 8
HID = 512
HC = HID // P
EPS = 1e-5
NEG_BIG = -1e38
MASKED = -3e38

(LN1_W, LN1_B, LN2_W, LN2_B, DECAY, FIRST, TMK, TMV, TMR, F_TMK, F_TMR) = range(11)
VECTORS = 11
PROJ = ("k", "v", "r", "o", "fr")

PAIRS = HC // 2
CUT = 3
SPLIT = (("PV", "PV"), ("PV", "PV"), ("PV", "PV"), ("PV", "AP"),
         ("AV", "AP"), ("AV", "AP"), ("AV", "AP"), ("AV", "AP"))


def pair_count(rounds, takes, e=EXP, j=0):
    flat = [how for pairs in SPLIT for how in pairs][:e * PAIRS + j]
    return sum(rounds in (None, r) and takes in (None, t) for r, t in flat)


EVENTS = dict(
    up_done=EXP * HC, y_done=EXP, k_ps=1, v_ps=1, r_ps=1, xnT_ps=1, zT_ps=1, router_ps=1, logit_ps=1, wT_ps=1,
    o_ps=1, h2T_ps=1, fr_ps=1, fk_ps=HC, fv_ps=1, fin_ps=1,
    gelu_done=EXP * HC, k_sb=1, v_sb=1, h1_ready=1, logitT_sb=1, exp_done=1, rt_ready=1, ed_ready=1, wT_sb=1,
    h2_ready=1, th_ready=1, x_hi_ready=1, act_hi=pair_count("A", None), relu_done=HC, kk_ready=HC,
    y_taken=EXP, xsplit=1, dve_lo=pair_count(None, "V"), stat1=1, norm1=1, mix1=1, args_ready=1, logit_sb=1, ed_arg=1, w_ready=1,
    rw_ready=1, bb_ready=1, x1_ready=1, stat2=1, norm2=1, mix2=1, fin_ready=1, out_ready=1,
    moe_added=EXP - 1, rstd1=1, rstd2=1, n2_ready=1, den_ready=1, xs_ready=1,
    pool_hi=pair_count("P", None), pool_lo=pair_count(None, "P"),
    x_loaded=16, w_stored=16, w_spread_a=16, w_spread_b=16, out_stored=16,
)

AHEAD = dict(
    tensor=("fin_ps", "fk_ps", "fv_ps", "o_ps"), vector=("fin_ready", "mix2", "out_ready"),
    gpsimd=("moe_added",), sync=("out_stored",),
)


def build(nc, x, vec, projs, fk, fv, wr, w1, b1, w2, b2, out):
    f32, f32r = mybir.dt.float32, mybir.dt.float32r
    ALU, ACT, AX = mybir.AluOpType, mybir.ActivationFunctionType, mybir.AxisListType

    ctx = ExitStack()
    with ctx:
        def sb(name, shape, dt=f32):
            return ctx.enter_context(nc.sbuf_tensor(name, shape, dt))

        def sem(name):
            return ctx.enter_context(nc.semaphore(name))

        vec_sb = sb("vec_sb", [P, VECTORS])
        negw = sb("negw", [P, 1])
        proj_sb = sb("proj_sb", [P, len(PROJ), P])
        fk_sb = sb("fk_sb", [P, HID])
        fv_sb = sb("fv_sb", [P, HC, P])
        wr_sb = sb("wr_sb", [P, EXP])
        wr_hi, wr_lo = sb("wr_hi", [P, EXP], f32r), sb("wr_lo", [P, EXP], f32r)
        w1_hi, w1_lo = sb("w1_hi", [P, EXP, HID], f32r), sb("w1_lo", [P, EXP, HID], f32r)
        w2_hi, w2_lo = sb("w2_hi", [P, EXP, HID], f32r), sb("w2_lo", [P, EXP, HID], f32r)
        b1_sb = sb("b1_sb", [P, EXP, HC])
        b2_sb = sb("b2_sb", [P, EXP])
        ident = sb("ident", [P, P])
        rank = sb("rank", [P, EXP])
        neg_half, euler = sb("neg_half", [P, NT]), sb("euler", [P, NT])

        x_tok = [sb(f"x_tok{i}", [P, NT, CH]) for i in range(2)]
        xn_tok = [sb(f"xn_tok{i}", [P, NT, CH]) for i in range(2)]
        z_tok = sb("z_tok", [P, NT, CH])
        x1_tok = sb("x1_tok", [P, NT, CH])
        z2_tok = z_tok
        xs_tok = sb("xs_tok", [P, NT, CH])
        bn1, bn2 = sb("bn1", [P, NT, 6]), sb("bn2", [P, NT, 6])
        mv1, mv2 = sb("mv1", [P, NT, 2]), sb("mv2", [P, NT, 2])
        ve1, ve2 = sb("ve1", [P, NT]), sb("ve2", [P, NT])
        ra, rb, rz = sb("ra", [P, NT]), sb("rb", [P, NT]), sb("rz", [P, NT])
        r2 = sb("r2", [P, NT])

        lg = sb("lg", [P, NT, EXP])
        lg2 = sb("lg2", [P, NT, EXP])
        eq, tie = sb("eq", [P, NT, EXP]), sb("tie", [P, NT, EXP])
        eq2, tie2 = sb("eq2", [P, NT, EXP]), sb("tie2", [P, NT, EXP])
        pick1, pick2 = sb("pick1", [P, NT, EXP]), sb("pick2", [P, NT, EXP])
        m1, m2 = sb("m1", [P, NT]), sb("m2", [P, NT])
        f1, f2 = sb("f1", [P, NT]), sb("f2", [P, NT])
        gap, ed = sb("gap", [P, NT]), sb("ed", [P, NT])
        dn, g1, g2 = sb("dn", [P, NT]), sb("g1", [P, NT]), sb("g2", [P, NT])
        wa, wb = sb("wa", [P, NT, EXP]), sb("wb", [P, NT, EXP])
        w_tok = sb("w_tok", [P, NT, EXP])
        wT = sb("wT", [EXP, TOK])
        logitT = wT
        w_bc = sb("w_bc", [P, EXP, TOK])

        x_hi = [sb(f"x_hi{i}", [P, TOK], f32r) for i in range(2)]
        x_lo = [sb(f"x_lo{i}", [P, TOK], f32r) for i in range(2)]
        h1 = [sb(f"h1_{i}", [P, 1 + TOK]) for i in range(2)]
        h2 = [sb(f"h2_{i}", [P, 1 + TOK]) for i in range(2)]
        dif = sb("dif", [P, TOK])
        xk, xv, xr = (sb(n, [P, TOK]) for n in ("xk", "xv", "xr"))
        kT, vT = sb("kT", [P, TOK]), sb("vT", [P, TOK])
        rt = kT
        pp, aa, bb = (sb(n, [P, 1 + TOK]) for n in ("pp", "aa", "bb"))
        ex = sb("ex", [P, 4, TOK])
        E1B, E2B, E1, E2 = range(4)
        n2, num, den, rw = (sb(n, [P, TOK]) for n in ("n2", "num", "den", "rw"))
        e2v, th, fin, pm = rw, n2, num, den
        xk2, xr2 = den, rw
        kk = ex
        g_raw = sb("g_raw", [P, HC, TOK])
        g_hi, g_lo = sb("g_hi", [P, 2, HC, TOK], f32r), sb("g_lo", [P, 2, HC, TOK], f32r)
        y_w = sb("y_w", [P, 2, TOK])
        moe = sb("moe", [P, 2, TOK])
        gated = th

        def bank(name):
            return ctx.enter_context(nc.psum_tensor(name, [P, TOK], f32))

        H = [bank(f"ps_h{i}") for i in range(3)]
        Y = bank("ps_y")
        A = [bank(f"ps_a{i}") for i in range(4)]
        FK_BANKS = (2, 3, 1, 2)

        w_dram = nc.dram_tensor("w_scratch", [CHUNKS, EXP, TOK], f32, kind="Internal").ap()
        x_t = x.rearrange("(q n p) c -> q p n c", n=NT, p=P)
        out_t = out.rearrange("(q n p) c -> q p n c", n=NT, p=P)

        S = {name: sem(name) for name in EVENTS}
        vec_in, wr_in, late_in = sem("vec_in"), sem("wr_in"), sem("late_in")
        const_ready, dve_const, negw_ready = sem("const_ready"), sem("dve_const"), sem("negw_ready")
        wr_rounded, wr_split = sem("wr_rounded"), sem("wr_split")

        UNITS = 2 * EXP
        unit_in = [sem(f"unit_in{u}") for u in range(UNITS)]
        roundings, logit_turns = sem("roundings"), sem("logit_turns")
        unit_rounded, unit_split = sem("unit_rounded"), sem("unit_split")

        def unit_raw(u):
            return ex[:, u % 12, :] if u % 12 < 4 else w_bc[:, u - 4, :]

        def unit_part(u, w1_part, w2_part):
            return (w2_part if u % 2 else w1_part)[:, u // 2, :]
        dve_step, pool_step, act_step = sem("dve_step"), sem("pool_step"), sem("act_step")

        def until_hi(eng, b, off, e, j):
            by = SPLIT[e][j][0]
            until(eng, {"A": "act_hi", "P": "pool_hi"}[by], b, off, pair_count(by, None, e, j) + 1)

        def until_lo(eng, b, off, e, j):
            by = SPLIT[e][j][1]
            until(eng, {"V": "dve_lo", "P": "pool_lo"}[by], b, off, pair_count(None, by, e, j) + 1)

        def until(eng, name, b, off, k):
            n = EVENTS[name]
            least = n * off + k
            ahead = n if any(name in names for names in AHEAD.values()) else 0
            if isinstance(b, int):
                if PAIR * n * b + least > 0:
                    eng.wait_ge(S[name], PAIR * n * b + least + ahead)
            else:
                assert least + ahead > 0, (name, off, k)
                eng.wait_ge(S[name], b * (PAIR * n) + (least + ahead))

        def signal_ahead(eng, which):
            for name in AHEAD[which]:
                eng.sem_inc(S[name], EVENTS[name])

        half_step = [0]

        def steps(eng, own):
            count = [0]

            def step(ins):
                count[0] += 1
                ins.then_inc(own, 1)
                return count[0]

            def after(n):
                if n:
                    eng.wait_ge(own, n)

            def restart():
                if count[0]:
                    eng.wait_ge(own, count[0])
                    eng.sem_clear(own)
                    count[0] = 0
                    half_step[0] = 0
            return step, after, restart

        def schedule(eng, slot, restart=None):
            for e in range(CUT):
                slot(0, 0, e)
            if restart:
                restart()
            with eng.Fori(0, CHUNKS // PAIR - 1) as b:
                for off, es in ((0, range(CUT, EXP)), (1, range(EXP)), (2, range(CUT))):
                    for e in es:
                        slot(b, off, e)
                if restart:
                    restart()
            last = CHUNKS // PAIR - 1
            for off, es in ((0, range(CUT, EXP)), (1, range(EXP))):
                for e in es:
                    slot(last, off, e)

        def has(b, off):
            return not isinstance(b, int) or 0 <= PAIR * b + off < CHUNKS

        def bcast(t):
            return t[:].rearrange("p (n o) -> p n o", o=1).to_broadcast([P, NT, EXP])

        block = ctx.enter_context(nc.Block())

        @block.sync
        def _(sp):
            signal_ahead(sp, "sync")
            sp.dma_start(x_tok[0][:], x_t[0]).then_inc(S["x_loaded"], 16)
            sp.dma_start(vec_sb[:], vec).then_inc(vec_in, 16)
            sp.dma_start(wr_sb[:], wr).then_inc(wr_in, 16)

            def load_unit(u):
                sp.dma_start(unit_raw(u), unit_part(u, w1, w2)).then_inc(unit_in[u], 16)

            def spread(q, half):
                name = ("w_spread_a", "w_spread_b")[half]
                until(sp, "y_taken", 0, q - 1, EXP // 2 * (half + 1))
                es = slice(half * EXP // 2, (half + 1) * EXP // 2)
                sp.dma_start(w_bc[:, es, :], w_dram[q:q + 1, es, :].to_broadcast([P, EXP // 2, TOK]))\
                  .then_inc(S[name], 16)

            def keep_w(q):
                until(sp, "wT_sb", 0, q, 1)
                sp.dma_start(w_dram[q], wT[:]).then_inc(S["w_stored"], 16)
                until(sp, "w_stored", 0, q, 16)

            def load(q):
                until(sp, "xs_ready", 0, q - 2, 1)
                until(sp, "x_loaded", 0, q - 1, 16)
                sp.dma_start(x_tok[q % 2][:], x_t[q]).then_inc(S["x_loaded"], 16)

            def store(q):
                until(sp, "out_ready", 0, q, 1)
                sp.dma_start(out_t[q], xs_tok[:]).then_inc(S["out_stored"], 16)

            for u in range(2):
                load_unit(u)
            sp.dma_start(b1_sb[:], b1).then_inc(vec_in, 16)
            sp.dma_start(b2_sb[:], b2).then_inc(vec_in, 16)
            for u in range(2, 8):
                load_unit(u)
            load(1)
            for u in range(8, 12):
                load_unit(u)
            for u in range(12, UNITS):
                sp.wait_ge(unit_split, u - 12 + 1)
                load_unit(u)
            keep_w(0)
            sp.wait_ge(unit_split, 8)
            spread(0, 0)
            sp.wait_ge(unit_split, 12)
            spread(0, 1)
            for q in range(CHUNKS):
                if q > 0:
                    store(q - 1)
                if q + 1 < CHUNKS:
                    if q + 2 < CHUNKS:
                        load(q + 2)
                    keep_w(q + 1)
                    spread(q + 1, 0)
                    spread(q + 1, 1)
            store(CHUNKS - 1)
            until(sp, "out_stored", 0, CHUNKS - 1, 16)

        @block.tensor
        def _(pe):
            def split_mm(dst, w_h, w_l, a_h, a_l):
                nc.tensor.matmul(dst, w_h, a_h, start=True, stop=False)
                nc.tensor.matmul(dst, w_h, a_l, start=False, stop=False)
                return nc.tensor.matmul(dst, w_l, a_h, start=False, stop=True)

            def up(b, off, e):
                for m in range(HC):
                    i = HC * e + m
                    if i == 0:
                        until(pe, "xsplit", b, off, 1)
                    if i >= 3:
                        until(pe, "gelu_done", b, off, i - 2)
                    else:
                        until(pe, "gelu_done", b, off - 1, (31, 32, 30)[i])
                    cols = slice(m * P, (m + 1) * P)
                    split_mm(H[i % 3][:], w1_hi[:, e, cols], w1_lo[:, e, cols], x_hi[off % 2][:],
                             x_lo[off % 2][:]).then_inc(S["up_done"], 1)

            def down(b, off, e):
                until(pe, "y_taken", b, off, e)
                for m in range(HC):
                    if m % 2 == 0:
                        until_lo(pe, b, off, e, m // 2)
                    w_h, w_l = (t[:, e, m * P:(m + 1) * P] for t in (w2_hi, w2_lo))
                    nc.tensor.matmul(Y[:], w_h, g_hi[:, e % 2, m, :], start=(m == 0), stop=False)
                    nc.tensor.matmul(Y[:], w_h, g_lo[:, e % 2, m, :], start=False, stop=False)
                    last = nc.tensor.matmul(Y[:], w_l, g_hi[:, e % 2, m, :], start=False, stop=(m == HC - 1))
                last.then_inc(S["y_done"], 1)

            def turn(dst, src, name):
                for n in range(NT):
                    last = nc.tensor.transpose(dst[:, n * P:(n + 1) * P], src(n), ident[:])
                last.then_inc(S[name], 1)

            def front(b, off):
                until(pe, "norm1", b, off, 1)
                until(pe, "relu_done", b, off - 2, HC)
                turn(A[2], lambda n: xn_tok[off % 2][:, n, :], "xnT_ps")
                turn(A[3], lambda n: z_tok[:, n, :], "zT_ps")

            def router(b, off):
                until(pe, "xsplit", b, off, 1)
                until(pe, "out_ready", b, off - 2, 1)
                split_mm(A[1][0:EXP, :], wr_hi[:], wr_lo[:], x_hi[off % 2][:], x_lo[off % 2][:])\
                    .then_inc(S["router_ps"], 1)

            def turn_logits(b, off):
                until(pe, "logitT_sb", b, off, 1)
                pe.sem_inc(logit_turns, 1)
                for n in range(NT):
                    last = nc.tensor.transpose(A[1][:, n * EXP:(n + 1) * EXP], logitT[:, n * P:(n + 1) * P],
                                               ident[0:EXP, 0:EXP])
                last.then_inc(S["logit_ps"], 1)

            def turn_w(b, off):
                until(pe, "w_ready", b, off, 1)
                for n in range(NT):
                    last = nc.tensor.transpose(A[1][0:EXP, n * P:(n + 1) * P], w_tok[:, n, :], ident[:])
                last.then_inc(S["wT_ps"], 1)

            def channel_out(b, off):
                until(pe, *(("v_sb", b, off + 1, 1) if has(b, off + 1) else ("relu_done", b, off, HC - 1)))
                for j in range(HC):
                    until(pe, "kk_ready", b, off, j + 1)
                    last = nc.tensor.matmul(A[1][:], fv_sb[:, j, :], kk[:, j, :], start=(j == 0), stop=(j == HC - 1))
                last.then_inc(S["fv_ps"], 1)

            def finish_turn(b, off):
                until(pe, "fin_ready", b, off, 1)
                turn(A[1], lambda n: fin[:, n * P:(n + 1) * P], "fin_ps")

            def slot(b, off, e):
                first = isinstance(b, int) and PAIR * b + off == 0
                if first:
                    pe.wait_ge(unit_split, 2 * (e + 1) + 1)
                if e + 1 < EXP:
                    up(b, off, e + 1)
                elif has(b, off + 1):
                    up(b, off + 1, 0)
                if e == 0:
                    if first:
                        pe.wait_ge(late_in, 16 * 3)
                    until(pe, "mix1", b, off, 1)
                    until(pe, "th_ready", b, off - 1, 1)
                    nc.tensor.matmul(A[0][:], proj_sb[:, 0, :], xk[:], start=True, stop=True).then_inc(S["k_ps"], 1)
                    until(pe, "relu_done", b, off - 1, HC - 1)
                    nc.tensor.matmul(A[1][:], proj_sb[:, 1, :], xv[:], start=True, stop=True).then_inc(S["v_ps"], 1)
                if e == 2 and not first:
                    finish_turn(b, off - 1)
                if e == 4 and has(b, off + 1):
                    router(b, off + 1)
                if e == 6:
                    until(pe, "norm2", b, off, 1)
                    until(pe, *(("h1_ready", b, off + 1, 1) if has(b, off + 1)
                                else ("relu_done", b, off - 1, HC)))
                    turn(A[3], lambda n: z2_tok[:, n, :], "h2T_ps")
                if e == 7:
                    if has(b, off + 1):
                        turn_w(b, off + 1)
                    until(pe, "mix2", b, off, 1)
                    until(pe, "x1_ready", b, off, 1)
                    nc.tensor.matmul(A[0][:], proj_sb[:, 4, :], xr2[:], start=True, stop=True).then_inc(S["fr_ps"], 1)
                    for j in range(HC):
                        if j == 0:
                            until(pe, *(("xsplit", b, off + 1, 1) if has(b, off + 1)
                                        else ("relu_done", b, off - 1, HC)))
                        if j == 1:
                            until(pe, "h2_ready", b, off, 1)
                        if j == 2:
                            until(pe, *(("wT_sb", b, off + 1, 1) if has(b, off + 1)
                                        else ("out_ready", b, off - 1, 1)))
                        if j == 3:
                            until(pe, "relu_done", b, off, 1)
                        nc.tensor.matmul(A[FK_BANKS[j]][:], fk_sb[:, j * P:(j + 1) * P], xk2[:],
                                         start=True, stop=True).then_inc(S["fk_ps"], 1)

                if first:
                    pe.wait_ge(unit_split, 2 * e + 2)
                down(b, off, e)

                if e == 0 and not first:
                    channel_out(b, off - 1)
                if e == 1:
                    until(pe, "k_sb", b, off, 1)
                    nc.tensor.matmul(A[0][:], proj_sb[:, 2, :], xr[:], start=True, stop=True).then_inc(S["r_ps"], 1)
                    if has(b, off + 1):
                        front(b, off + 1)
                if e == 4:
                    if has(b, off + 1):
                        turn_logits(b, off + 1)
                    until(pe, "rw_ready", b, off, 1)
                    for n in range(NT):
                        last = nc.tensor.matmul(A[0][:, n * P:(n + 1) * P], rw[:, n * P:(n + 1) * P], proj_sb[:, 3, :],
                                                start=True, stop=True)
                    last.then_inc(S["o_ps"], 1)
                if first and e == CUT - 1:
                    pe.wait_ge(unit_split, UNITS)

            signal_ahead(pe, "tensor")
            pe.wait_ge(const_ready, 2)
            front(0, 0)
            pe.wait_ge(wr_split, 1)
            router(0, 0)
            pe.wait_ge(unit_split, 1)
            up(0, 0, 0)
            turn_logits(0, 0)
            turn_w(0, 0)
            schedule(pe, slot)
            last = CHUNKS // PAIR - 1
            channel_out(last, 1)
            finish_turn(last, 1)

        @block.scalar
        def _(act):
            act.dma_start(proj_sb[:], projs).then_inc(late_in, 16)
            act.dma_start(fk_sb[:], fk).then_inc(late_in, 16)
            act.dma_start(fv_sb[:], fv).then_inc(late_in, 16)

            def gelu(b, off, e):
                def round_pair(j):
                    until(act, "gelu_done", b, off, HC * e + 2 * j + 2)
                    until(act, "y_done", b, off, e - 1)
                    nc.scalar.activation(g_hi[:, e % 2, 2 * j:2 * j + 2, :], g_raw[:, 2 * j:2 * j + 2, :], ACT.Copy)\
                      .then_inc(S["act_hi"], 1)

                for m in range(HC):
                    i = HC * e + m
                    if m % 2 == 0:
                        until_lo(act, b, off if e else off - 1, (e - 1) % EXP, m // 2)
                    until(act, "up_done", b, off, i + 1)
                    nc.scalar.activation(g_raw[:, m, :], H[i % 3][:], ACT.Gelu,
                                         bias=b1_sb[:, e, m:m + 1]).then_inc(S["gelu_done"], 1)
                    if m == 2 and SPLIT[e][0][0] == "A":
                        round_pair(0)
                if SPLIT[e][1][0] == "A":
                    round_pair(1)

            def scaled(b, off, h, src, w_col, b_col, name, freed):
                until(act, freed, b, off - 1, 1)
                if off % 2 == 1:
                    until(act, name, b, off - 1, 1)
                    nc.scalar.activation(h[1][:, 0:1], h[0][:, TOK:TOK + 1], ACT.Copy)
                nc.scalar.activation(h[off % 2][:, 1:1 + TOK], src, ACT.Identity, bias=vec_sb[:, b_col:b_col + 1],
                                     scale=vec_sb[:, w_col:w_col + 1]).then_inc(S[name], 1)

            def front(b, off):
                until(act, "xnT_ps", b, off, 1)
                until(act, "up_done", b, off - 2, EXP * HC)
                nc.scalar.activation(x_hi[off % 2][:], A[2][:], ACT.Copy).then_inc(S["x_hi_ready"], 1)
                until(act, "zT_ps", b, off, 1)
                scaled(b, off, h1, A[3][:], LN1_W, LN1_B, "h1_ready", "mix1")

            def take_logits(b, off):
                until(act, "router_ps", b, off, 1)
                until(act, "w_stored", b, off - 1, 16)
                nc.scalar.activation(logitT[:], A[1][0:EXP, :], ACT.Copy).then_inc(S["logitT_sb"], 1)

            def take_w(b, off):
                until(act, "wT_ps", b, off, 1)
                nc.scalar.activation(wT[:], A[1][0:EXP, :], ACT.Copy).then_inc(S["wT_sb"], 1)

            def slot(b, off, e):
                if e + 1 < EXP:
                    gelu(b, off, e + 1)
                elif has(b, off + 1):
                    gelu(b, off + 1, 0)
                if e == 0:
                    until(act, "k_ps", b, off, 1)
                    until(act, "rw_ready", b, off - 1, 1)
                    nc.scalar.activation(kT[:], A[0][:], ACT.Copy).then_inc(S["k_sb"], 1)
                    until(act, "v_ps", b, off, 1)
                    nc.scalar.activation(vT[:], A[1][:], ACT.Copy).then_inc(S["v_sb"], 1)
                if e == 1:
                    until(act, "args_ready", b, off, 1)
                    nc.scalar.activation(ex[:], ex[:], ACT.Exp).then_inc(S["exp_done"], 1)
                if e == 2:
                    until(act, "r_ps", b, off, 1)
                    until(act, "args_ready", b, off, 1)
                    nc.scalar.activation(rt[:], A[0][:], ACT.Tanh, scale=0.5).then_inc(S["rt_ready"], 1)
                    if has(b, off + 1):
                        front(b, off + 1)
                if e == 4 and has(b, off + 1):
                    take_logits(b, off + 1)
                if e == 6:
                    until(act, "h2T_ps", b, off, 1)
                    scaled(b, off, h2, A[3][:], LN2_W, LN2_B, "h2_ready", "mix2")
                if e == 7:
                    if has(b, off + 1):
                        take_w(b, off + 1)
                    until(act, "fr_ps", b, off, 1)
                    nc.scalar.activation(th[:], A[0][:], ACT.Tanh, scale=0.5).then_inc(S["th_ready"], 1)
                    until(act, "fv_ps", b, off - 1, 1)
                    for j in range(HC + 1):
                        if j < HC:
                            until(act, "fk_ps", b, off, j + 1)
                            nc.scalar.activation(kk[:, j, :], A[FK_BANKS[j]][:], ACT.Relu)\
                              .then_inc(S["relu_done"], 1)
                        if j > 0:
                            until(act, "relu_done", b, off, j)
                            nc.scalar.activation(kk[:, j - 1, :], kk[:, j - 1, :], ACT.Square)\
                              .then_inc(S["kk_ready"], 1)

            act.wait_ge(vec_in, 16 * 3)
            nc.scalar.activation(negw[:], vec_sb[:, DECAY:DECAY + 1], ACT.Exp).then_inc(act_step, 1)
            act.wait_ge(act_step, 1)
            nc.scalar.activation(negw[:], negw[:], ACT.Copy, scale=-1.0).then_inc(negw_ready, 1)
            act.wait_ge(dve_const, 2)
            front(0, 0)
            take_logits(0, 0)
            gelu(0, 0, 0)
            take_w(0, 0)
            schedule(act, slot)

        @block.vector
        def _(dve):
            V = nc.vector
            step, after, restart = steps(dve, dve_step)

            def stats(src, bn, mv, ve, name):
                for n in range(NT):
                    t = step(V.bn_stats(bn[:, n, :], src[:, n, :]))
                for n in range(NT):
                    after(t - NT + 1 + n)
                    u = step(V.bn_aggr(mv[:, n, :], bn[:, n, :]))
                after(u)
                V.tensor_scalar(ve[:].rearrange("p (n o) -> p n o", o=1), mv[:, :, 1:2], EPS, None, ALU.add)\
                 .then_inc(S[name], 1)

            def normalize(dst, src, mv, r):
                for n in range(NT):
                    last = V.tensor_scalar(dst[:, n, :], src[:, n, :], mv[:, n, 0:1], r[:, n:n + 1],
                                           ALU.subtract, ALU.mult)
                return last

            def front_stats(b, off):
                until(dve, "x_loaded", b, off, 16)
                stats(x_tok[off % 2], bn1, mv1, ve1, "stat1")

            def front_norm(b, off):
                until(dve, "rstd1", b, off, 1)
                until(dve, "h2T_ps", b, off - 2, 1)
                until(dve, "zT_ps", b, off - 1, 1)
                normalize(xn_tok[off % 2], x_tok[off % 2], mv1, ra)
                normalize(z_tok, x_tok[off % 2], mv1, rz).then_inc(S["norm1"], 1)

            def split_x(b, off):
                until(dve, "x_hi_ready", b, off, 1)
                V.tensor_tensor(x_lo[off % 2][:], A[2][:], x_hi[off % 2][:].bitcast(f32), ALU.subtract)\
                 .then_inc(S["xsplit"], 1)

            def split_g(b, off, e, j):
                if SPLIT[e][j][1] != "V":
                    return
                until_hi(dve, b, off, e, j)
                part = slice(2 * j, 2 * j + 2)
                V.tensor_tensor(g_lo[:, e % 2, part, :], g_raw[:, part, :], g_hi[:, e % 2, part, :].bitcast(f32),
                                ALU.subtract).then_inc(S["dve_lo"], 1)

            def mixes(h, diff, outs, name):
                now, before = h[:, 1:1 + TOK], h[:, 0:TOK]
                after(step(V.tensor_tensor(diff[:], now, before, ALU.subtract)))
                for dst, mu in outs:
                    last = V.scalar_tensor_tensor(out=dst[:], in0=diff[:], scalar=vec_sb[:, mu:mu + 1], in1=before,
                                                  op0=ALU.mult, op1=ALU.add)
                last.then_inc(S[name], 1)

            def mix1(b, off):
                until(dve, "h1_ready", b, off, 1)
                until(dve, "r_ps", b, off - 1, 1)
                until(dve, "mix2", b, off - 1, 1)
                mixes(h1[off % 2], dif, ((xk, TMK), (xv, TMV), (xr, TMR)), "mix1")

            def first_best(src, peak, same, tie_, f, pick):
                after(step(V.tensor_reduce(out=peak[:], in_=src[:], op=ALU.max, axis=AX.X)))
                after(step(V.tensor_tensor(same[:], src[:], bcast(peak), ALU.is_equal)))
                after(step(V.tensor_tensor(tie_[:], same[:], rank[:].rearrange("p (o e) -> p o e", o=1)
                                           .to_broadcast([P, NT, EXP]), ALU.mult)))
                after(step(V.tensor_reduce(out=f[:], in_=tie_[:], op=ALU.max, axis=AX.X)))
                after(step(V.tensor_tensor(pick[:], tie_[:], bcast(f), ALU.is_equal)))

            def choose(b, off):
                until(dve, "logit_ps", b, off, 1)
                V.tensor_copy(lg[:].rearrange("p n e -> p (n e)"), A[1][:, 0:NT * EXP]).then_inc(S["logit_sb"], 1)
                until(dve, "logit_sb", b, off, 1)
                first_best(lg, m1, eq, tie, f1, pick1)
                after(step(V.scalar_tensor_tensor(out=lg2[:], in0=pick1[:], scalar=MASKED, in1=lg[:],
                                                  op0=ALU.mult, op1=ALU.add)))

            def choose_second(b, off):
                first_best(lg2, m2, eq2, tie2, f2, pick2)
                V.tensor_tensor(gap[:], m2[:], m1[:], ALU.subtract).then_inc(S["ed_arg"], 1)

            def weigh(b, off):
                until(dve, "ed_ready", b, off, 1)
                after(step(V.tensor_scalar(dn[:], ed[:], 1.0, None, ALU.add)))
                after(step(V.reciprocal(g1[:], dn[:])))
                t = step(V.tensor_tensor(g2[:], ed[:], g1[:], ALU.mult))
                u = step(V.tensor_tensor(wa[:], pick1[:], bcast(g1), ALU.mult))
                after(t)
                v = step(V.tensor_tensor(wb[:], pick2[:], bcast(g2), ALU.mult))
                after(v)
                until(dve, "wT_ps", b, off - 1, 1)
                V.tensor_tensor(w_tok[:], wa[:], wb[:], ALU.add).then_inc(S["w_ready"], 1)

            def state_max(b, off):
                until(dve, "k_sb", b, off, 1)
                until(dve, "rw_ready", b, off - 1, 1)
                for t, start in ((pp, NEG_BIG), (aa, 0.0), (bb, 0.0)):
                    s = step(V.tensor_copy(t[:, 0:1], t[:, TOK:TOK + 1]) if off % 2 else V.memset(t[:, 0:1], start))
                after(s)
                half_step[0] = step(V.tensor_tensor_scan(
                    pp[:, 1:1 + TOK], negw[:, 0:1].to_broadcast([P, TOK]), kT[:], pp[:, 0:1], ALU.add, ALU.max))

            def state_args(b, off):
                before, now = pp[:, 0:TOK], pp[:, 1:1 + TOK]
                u = vec_sb[:, FIRST:FIRST + 1]
                until(dve, "fk_ps", b, off - 1, HC)
                after(half_step[0])
                m = step(V.scalar_tensor_tensor(out=pm[:], in0=kT[:], scalar=u, in1=before, op0=ALU.add, op1=ALU.max))
                until(dve, "fv_ps", b, off - 1, 1)
                V.scalar_tensor_tensor(out=ex[:, E1B, :], in0=before, scalar=negw[:, 0:1], in1=now,
                                       op0=ALU.add, op1=ALU.subtract)
                V.tensor_tensor(ex[:, E2B, :], kT[:], now, ALU.subtract)
                after(m)
                V.tensor_tensor(ex[:, E1, :], before, pm[:], ALU.subtract)
                V.scalar_tensor_tensor(out=ex[:, E2, :], in0=kT[:], scalar=u, in1=pm[:],
                                       op0=ALU.add, op1=ALU.subtract).then_inc(S["args_ready"], 1)

            def scan_weights(b, off):
                until(dve, "exp_done", b, off, 1)
                until(dve, "v_sb", b, off, 1)
                until(dve, "fr_ps", b, off - 1, 1)
                V.tensor_tensor_scan(bb[:, 1:1 + TOK], ex[:, E1B, :], ex[:, E2B, :], bb[:, 0:1],
                                     ALU.mult, ALU.add).then_inc(S["bb_ready"], 1)
                half_step[0] = step(V.tensor_tensor(e2v[:], ex[:, E2B, :], vT[:], ALU.mult))

            def scan_values(b, off):
                after(half_step[0])
                after(step(V.tensor_tensor_scan(aa[:, 1:1 + TOK], ex[:, E1B, :], e2v[:], aa[:, 0:1],
                                                ALU.mult, ALU.add)))
                until(dve, "fin_ps", b, off - 1, 1)
                half_step[0] = step(V.tensor_tensor(num[:], ex[:, E1, :], aa[:, 0:TOK], ALU.mult))

            HALVES = (slice(0, TOK // 2), slice(TOK // 2, TOK))

            def receptance(b, off):
                until(dve, "rt_ready", b, off, 1)
                until(dve, "n2_ready", b, off, 1)
                after(half_step[0])
                after(step(V.tensor_tensor(num[:], num[:], n2[:], ALU.add)))
                half_step[0] = step(V.scalar_tensor_tensor(out=num[:], in0=rt[:], scalar=1.0, in1=num[:],
                                                           op0=ALU.add, op1=ALU.mult))

            def receptance_half(b, off):
                until(dve, "den_ready", b, off, 1)
                step(V.reciprocal(den[:, HALVES[0]], den[:, HALVES[0]]))

            def receptance_rest(b, off):
                t = step(V.reciprocal(den[:, HALVES[1]], den[:, HALVES[1]]))
                after(t)
                V.scalar_tensor_tensor(out=rw[:], in0=num[:], scalar=0.5, in1=den[:], op0=ALU.mult, op1=ALU.mult)\
                 .then_inc(S["rw_ready"], 1)

            def take_y(b, off, e):
                if e % (EXP // 2) == 0:
                    until(dve, ("w_spread_a", "w_spread_b")[e // (EXP // 2)], b, off, 16)
                if e == 0:
                    until(dve, "fin_ready", b, off - 2, 1)
                until(dve, "y_done", b, off, e + 1)
                if e == 2:
                    until(dve, "moe_added", b, off - 1, EXP - 1)
                if e >= 3:
                    until(dve, "moe_added", b, off, e - 2)
                dst = moe[:, off % 2, :] if e == 0 else y_w[:, e % 2, :]
                V.scalar_tensor_tensor(out=dst, in0=Y[:], scalar=b2_sb[:, e:e + 1], in1=w_bc[:, e, :],
                                       op0=ALU.add, op1=ALU.mult).then_inc(S["y_taken"], 1)

            def finish_gate(b, off):
                until(dve, "fv_ps", b, off, 1)
                until(dve, "th_ready", b, off, 1)
                after(step(V.scalar_tensor_tensor(out=gated[:], in0=th[:], scalar=1.0, in1=A[1][:],
                                                  op0=ALU.add, op1=ALU.mult)))
                until(dve, "moe_added", b, off, EXP - 1)
                until(dve, "rw_ready", b, off, 1)
                V.scalar_tensor_tensor(out=fin[:], in0=gated[:], scalar=0.5, in1=moe[:, off % 2, :],
                                       op0=ALU.mult, op1=ALU.add).then_inc(S["fin_ready"], 1)

            def finish_out(b, off):
                until(dve, "fin_ps", b, off, 1)
                until(dve, "xs_ready", b, off, 1)
                V.tensor_tensor(xs_tok[:].rearrange("p n c -> p (n c)"), A[1][:],
                                xs_tok[:].rearrange("p n c -> p (n c)"), ALU.add).then_inc(S["out_ready"], 1)

            def slot(b, off, e):
                first = isinstance(b, int) and PAIR * b + off == 0
                ahead = has(b, off + 1)
                nxt = (b, off, e + 1) if e + 1 < EXP else (b, off + 1, 0) if ahead else None

                if e == 0 and ahead:
                    front_stats(b, off + 1)
                if e == 1:
                    state_args(b, off)
                if e == 3 and ahead:
                    split_x(b, off + 1)
                if e == 4:
                    receptance_rest(b, off)
                if e == 5:
                    until(dve, "o_ps", b, off, 1)
                    V.tensor_tensor(x1_tok[:].rearrange("p n c -> p (n c)"), A[0][:],
                                    xn_tok[off % 2][:].rearrange("p n c -> p (n c)"), ALU.add).then_inc(S["x1_ready"], 1)
                    until(dve, "x1_ready", b, off, 1)
                    stats(x1_tok, bn2, mv2, ve2, "stat2")
                if e == 7 and ahead:
                    mix1(b, off + 1)

                if nxt:
                    split_g(*nxt, 0)

                if e == 2 and not first:
                    finish_out(b, off - 1)
                if e == 3:
                    receptance(b, off)
                if e == 6 and ahead:
                    weigh(b, off + 1)

                if nxt:
                    split_g(*nxt, 1)

                if e == 0:
                    state_max(b, off)
                    if ahead:
                        front_norm(b, off + 1)
                if e == 1 and not first:
                    finish_gate(b, off - 1)
                if e == 2:
                    scan_weights(b, off)
                    scan_values(b, off)
                if e == 3:
                    receptance_half(b, off)
                if e == 4 and ahead:
                    choose(b, off + 1)
                    choose_second(b, off + 1)
                if e == 5:
                    until(dve, "rstd2", b, off, 1)
                    if ahead:
                        until(dve, "zT_ps", b, off + 1, 1)
                    normalize(z2_tok, x1_tok, mv2, r2).then_inc(S["norm2"], 1)
                if e == 6:
                    until(dve, "h2_ready", b, off, 1)
                    until(dve, "mix1", b, off, 1)
                    mixes(h2[off % 2], dif, ((xr2, F_TMR), (xk2, F_TMK)), "mix2")
                take_y(b, off, e)

            def split_unit(u):
                dve.wait_ge(unit_rounded, u + 1)
                V.tensor_tensor(unit_part(u, w1_lo, w2_lo), unit_raw(u), unit_part(u, w1_hi, w2_hi).bitcast(f32),
                                ALU.subtract).then_inc(unit_split, 1)

            signal_ahead(dve, "vector")
            for t in (h1[0], h2[0]):
                V.memset(t[:, 0:1], 0.0).then_inc(dve_const, 1)
            front_stats(0, 0)
            dve.wait_ge(wr_rounded, 1)
            V.tensor_tensor(wr_lo[:], wr_sb[:], wr_hi[:].bitcast(f32), ALU.subtract).then_inc(wr_split, 1)
            front_norm(0, 0)
            split_unit(0)
            split_x(0, 0)
            split_unit(1)
            choose(0, 0)
            choose_second(0, 0)
            split_unit(2)
            split_unit(3)
            weigh(0, 0)
            split_g(0, 0, 0, 0)
            split_g(0, 0, 0, 1)
            for u in range(4, 8):
                split_unit(u)
            mix1(0, 0)
            for u in range(8, 12):
                split_unit(u)
            for u in range(12, UNITS):
                split_unit(u)
            dve.wait_ge(negw_ready, 1)
            schedule(dve, slot, restart)
            last = CHUNKS // PAIR - 1
            finish_gate(last, 1)
            finish_out(last, 1)

        @block.gpsimd
        def _(pool):
            G = nc.gpsimd
            step, after, restart = steps(pool, pool_step)

            def add_y(b, off, e):
                until(pool, "y_taken", b, off, e + 1)
                if e > 1:
                    until(pool, "moe_added", b, off, e - 1)
                acc = moe[:, off % 2, :]
                G.tensor_tensor(acc, acc, y_w[:, e % 2, :], ALU.add)\
                 .then_inc(S["moe_added"], 1)

            def roots1(b, off):
                until(pool, "stat1", b, off, 1)
                until(pool, "norm1", b, off - 1, 1)
                var = mv1[:, :, 1:2].rearrange("p n o -> p (n o)")
                after(step(G.tensor_tensor(ra[:], ve1[:], neg_half[:], ALU.pow)))
                after(step(G.tensor_tensor(rb[:], ra[:], ra[:], ALU.mult)))
                after(step(G.tensor_tensor(rb[:], rb[:], var, ALU.mult)))
                after(step(G.tensor_scalar(rb[:], rb[:], EPS, None, ALU.add)))
                after(step(G.tensor_tensor(rb[:], rb[:], neg_half[:], ALU.pow)))
                G.tensor_tensor(rz[:], ra[:], rb[:], ALU.mult).then_inc(S["rstd1"], 1)

            def round_g(b, off, e, j):
                part = slice(2 * j, 2 * j + 2)
                if SPLIT[e][j][0] == "P":
                    until(pool, "gelu_done", b, off, HC * e + 2 * j + 2)
                    until(pool, "y_done", b, off, e - 1)
                    pool.sem_inc(roundings, 1)
                    G.tensor_scalar(g_hi[:, e % 2, part, :], g_raw[:, part, :], 1.0, 0.0, ALU.mult, ALU.add)\
                     .then_inc(S["pool_hi"], 1)
                if SPLIT[e][j][1] == "P":
                    until_hi(pool, b, off, e, j)
                    G.tensor_tensor(g_lo[:, e % 2, part, :], g_raw[:, part, :], g_hi[:, e % 2, part, :].bitcast(f32),
                                    ALU.subtract).then_inc(S["pool_lo"], 1)

            def exp_gap(b, off):
                until(pool, "ed_arg", b, off, 1)
                G.tensor_tensor(ed[:], euler[:], gap[:], ALU.pow).then_inc(S["ed_ready"], 1)

            def slot(b, off, e):
                nxt = (b, off, e + 1) if e + 1 < EXP else (b, off + 1, 0) if has(b, off + 1) else None
                if e == 2:
                    until(pool, "exp_done", b, off, 1)
                    until(pool, "v_sb", b, off, 1)
                    until(pool, "fin_ready", b, off - 1, 1)
                    G.tensor_tensor(n2[:], ex[:, E2, :], vT[:], ALU.mult).then_inc(S["n2_ready"], 1)
                if e == 6 and has(b, off + 1):
                    exp_gap(b, off + 1)
                if nxt:
                    round_g(*nxt, 0)
                if e == 3:
                    until(pool, "bb_ready", b, off, 1)
                    after(step(G.tensor_tensor(den[:], ex[:, E1, :], bb[:, 0:TOK], ALU.mult)))
                    G.tensor_tensor(den[:], den[:], ex[:, E2, :], ALU.add).then_inc(S["den_ready"], 1)
                elif e >= 2:
                    if e == 5:
                        until(pool, "stat2", b, off, 1)
                        G.tensor_tensor(r2[:], ve2[:], neg_half[:], ALU.pow).then_inc(S["rstd2"], 1)
                    add_y(b, off, e - 1)
                elif e == 0 and not (isinstance(b, int) and PAIR * b + off == 0):
                    add_y(b, off - 1, EXP - 1)
                if nxt:
                    round_g(*nxt, 1)
                if e == 3:
                    add_y(b, off, e - 1)
                if e == 0 and has(b, off + 1):
                    roots1(b, off + 1)
                if e == 5:
                    until(pool, "out_stored", b, off - 1, 16)
                    G.tensor_tensor(xs_tok[:], x_tok[off % 2][:], x1_tok[:], ALU.add).then_inc(S["xs_ready"], 1)

            signal_ahead(pool, "gpsimd")
            step(G.memset(neg_half[:], -0.5))
            step(G.memset(euler[:], float(np.e)))
            step(G.memset(ident[:], 0.0))
            after(step(G.memset(rank[:], 0.0)))
            G.affine_select(out=ident[:], in_=ident[:], compare_op=ALU.not_equal, fill=1.0, base=0,
                            pattern=[[-1, P]], channel_multiplier=1).then_inc(const_ready, 1)
            for e in range(EXP):
                last = G.memset(rank[:, e:e + 1], float(EXP - e))
            last.then_inc(const_ready, 1)
            pool.wait_ge(wr_in, 16)
            G.tensor_scalar(wr_hi[:], wr_sb[:], 1.0, 0.0, ALU.mult, ALU.add).then_inc(wr_rounded, 1)
            roots1(0, 0)
            for u in range(UNITS):
                if u == 4:
                    exp_gap(0, 0)
                    round_g(0, 0, 0, 0)
                    round_g(0, 0, 0, 1)
                pool.wait_ge(unit_in[u], 16)
                G.tensor_scalar(unit_part(u, w1_hi, w2_hi), unit_raw(u), 1.0, 0.0, ALU.mult, ALU.add)\
                 .then_inc(unit_rounded, 1)
            schedule(pool, slot, restart)
            add_y(CHUNKS // PAIR - 1, 1, EXP - 1)


def kernel(L0_attn_x, L0_attn_ln1_w, L0_attn_ln1_b, L0_attn_ln2_w, L0_attn_ln2_b, L0_attn_time_decay,
           L0_attn_time_first, L0_attn_tmk, L0_attn_tmv, L0_attn_tmr, L0_attn_att_kw, L0_attn_att_vw,
           L0_attn_att_rw, L0_attn_att_ow, L0_attn_f_tmk, L0_attn_f_tmr, L0_attn_f_kw, L0_attn_f_rw,
           L0_attn_f_vw, L0_ffn_Wr, L0_ffn_W1, L0_ffn_b1, L0_ffn_W2, L0_ffn_b2):
    import concourse.bacc as bacc
    from concourse.bass_utils import run_bass_kernel_spmd

    def lay(a):
        return np.ascontiguousarray(a)

    a = np.asarray
    arrays = dict(
        x=lay(a(L0_attn_x).reshape(BATCH * TIME, CH)),
        vec=lay(np.stack([a(v) for v in (
            L0_attn_ln1_w, L0_attn_ln1_b, L0_attn_ln2_w, L0_attn_ln2_b, L0_attn_time_decay, L0_attn_time_first,
            L0_attn_tmk, L0_attn_tmv, L0_attn_tmr, L0_attn_f_tmk, L0_attn_f_tmr)], axis=1)),
        projs=lay(np.stack([a(w).T for w in (
            L0_attn_att_kw, L0_attn_att_vw, L0_attn_att_rw, L0_attn_att_ow, L0_attn_f_rw)], axis=1)),
        fk=lay(a(L0_attn_f_kw).T),
        fv=lay(a(L0_attn_f_vw).T.reshape(HC, P, CH).transpose(1, 0, 2)),
        wr=lay(a(L0_ffn_Wr).T),
        w1=lay(a(L0_ffn_W1).transpose(2, 0, 1)),
        b1=lay(a(L0_ffn_b1).reshape(EXP, HC, P).transpose(2, 0, 1)),
        w2=lay(a(L0_ffn_W2).transpose(0, 2, 1).reshape(EXP, HC, P, CH).transpose(2, 0, 1, 3).reshape(P, EXP, HID)),
        b2=lay(a(L0_ffn_b2).T),
    )
    nc = bacc.Bacc("TRN2", target_bir_lowering=False, num_devices=1)
    args = [nc.dram_tensor(n, v.shape, mybir.dt.from_np(v.dtype), kind="ExternalInput").ap() for n, v in arrays.items()]
    out = nc.dram_tensor("out", (BATCH * TIME, CH), mybir.dt.float32, kind="ExternalOutput").ap()
    build(nc, *args, out)
    r = run_bass_kernel_spmd(nc, [arrays], core_ids=[0])
    return r.results[0]["out"].reshape(BATCH, TIME, CH)
```

```python
import numpy as np
import concourse.bass as bass
from concourse import mybir
from contextlib import ExitStack

P = 128
BATCH, TIME, CH = 4, 1024, 128
TOK = 512
NT = TOK // P
CHUNKS = BATCH * TIME // TOK
PAIR = TIME // TOK
EXP = 8
HID = 512
HC = HID // P
EPS = 1e-5
NEG_BIG = -1e38
MASKED = -3e38

(LN1_W, LN1_B, LN2_W, LN2_B, DECAY, FIRST, TMK, TMV, TMR, F_TMK, F_TMR) = range(11)
VECTORS = 11
PROJ = ("k", "v", "r", "o", "fr")
KVR = 3

PAIRS = HC // 2
GROUP = 2
RING = 2 * GROUP
ADD_LATE = (3, 5)
CUT = 3

SPLIT = (("PV", "PV"), ("AV", "AV"), ("PV", "PV"), ("PV", "AP"),
         ("AV", "AP"), ("PV", "AP"), ("PV", "AV"), ("PV", "AP"))


def pair_count(rounds, takes, e=EXP, j=0):
    flat = [how for pairs in SPLIT for how in pairs][:e * PAIRS + j]
    return sum(rounds in (None, r) and takes in (None, t) for r, t in flat)


EVENTS = dict(
    up_done=EXP * HC, y_done=EXP, k_ps=1, v_ps=1, r_ps=1, xnT_ps=1, zT_ps=1, router_ps=1, logit_ps=1, wT_ps=1,
    o_ps=1, h2T_ps=1, fr_ps=1, fk_ps=HC, fv_ps=1, fin_ps=1,
    gelu_done=EXP * HC, k_sb=1, v_sb=1, h1_ready=1, logitT_sb=1, exp_done=1, rt_ready=1, wT_sb=1,
    h2_ready=1, th_ready=1, x_hi_ready=1, act_hi=pair_count("A", None), relu_done=HC, kk_ready=HC,
    y_taken=EXP, xsplit=1, dve_lo=pair_count(None, "V"), stat1=1, norm_x=1, norm1=1, mix1=1, args_ready=1,
    logit_sb=1, ed_arg=1, w_ready=1, rw_ready=1, bb_ready=1, x1_ready=1, stat2=1, norm2=1, mix2=1, xk2_split=1,
    fin_ready=1, out_ready=1,
    moe_added=EXP - 1, rstd_x=1, k_split=1, v_split=1, r_split=1, rstd1=1, rstd2=1, n2_ready=1, den_ready=1,
    xs_ready=1, ed_ready=1,
    pool_hi=pair_count("P", None), pool_lo=pair_count(None, "P"),
    x_loaded=16, w_stored=16, w_spread0=16, w_spread1=16, w_spread2=16, w_spread3=16, out_stored=16,
)

AHEAD = dict(
    tensor=("fin_ps", "fk_ps", "fv_ps", "o_ps"), vector=("fin_ready", "mix2", "out_ready"),
    gpsimd=("moe_added",), sync=("out_stored",),
)


def build(nc, x, vec, projs, fk, fv, wr, w1, b1, w2, b2, out):
    f32, f32r = mybir.dt.float32, mybir.dt.float32r
    ALU, ACT, AX = mybir.AluOpType, mybir.ActivationFunctionType, mybir.AxisListType

    ctx = ExitStack()
    with ctx:
        def sb(name, shape, dt=f32):
            return ctx.enter_context(nc.sbuf_tensor(name, shape, dt))

        def sem(name):
            return ctx.enter_context(nc.semaphore(name))

        vec_sb = sb("vec_sb", [P, VECTORS])
        negw = sb("negw", [P, 1])
        proj_sb = sb("proj_sb", [P, len(PROJ) - KVR, P])
        kvr_hi, kvr_lo = sb("kvr_hi", [P, KVR, P], f32r), sb("kvr_lo", [P, KVR, P], f32r)
        fk_hi, fk_lo = sb("fk_hi", [P, HID], f32r), sb("fk_lo", [P, HID], f32r)
        fv_sb = sb("fv_sb", [P, HC, P])
        wr_sb = sb("wr_sb", [P, EXP])
        wr_hi, wr_lo = sb("wr_hi", [P, EXP], f32r), sb("wr_lo", [P, EXP], f32r)
        w1_hi, w1_lo = sb("w1_hi", [P, EXP, HID], f32r), sb("w1_lo", [P, EXP, HID], f32r)
        w2_hi, w2_lo = sb("w2_hi", [P, EXP, HID], f32r), sb("w2_lo", [P, EXP, HID], f32r)
        b1_sb = sb("b1_sb", [P, EXP, HC])
        b2_sb = sb("b2_sb", [P, EXP])
        ident = sb("ident", [P, P])
        rank = sb("rank", [P, EXP])
        neg_half, euler = sb("neg_half", [P, NT]), sb("euler", [P, NT])

        x_tok = [sb(f"x_tok{i}", [P, NT, CH]) for i in range(2)]
        xn_tok = [sb(f"xn_tok{i}", [P, NT, CH]) for i in range(2)]
        z_tok = sb("z_tok", [P, NT, CH])
        x1_tok = sb("x1_tok", [P, NT, CH])
        z2_tok = z_tok
        xs_tok = sb("xs_tok", [P, NT, CH])
        bn1, bn2 = sb("bn1", [P, NT, 6]), sb("bn2", [P, NT, 6])
        mv1, mv2 = sb("mv1", [P, NT, 2]), sb("mv2", [P, NT, 2])
        ve1, ve2 = sb("ve1", [P, NT]), sb("ve2", [P, NT])
        ra, rb, rz = sb("ra", [P, NT]), sb("rb", [P, NT]), sb("rz", [P, NT])
        r2 = sb("r2", [P, NT])

        lg = sb("lg", [P, NT, EXP])
        lg2 = sb("lg2", [P, NT, EXP])
        eq, tie = sb("eq", [P, NT, EXP]), sb("tie", [P, NT, EXP])
        eq2, tie2 = sb("eq2", [P, NT, EXP]), sb("tie2", [P, NT, EXP])
        pick1, pick2 = sb("pick1", [P, NT, EXP]), sb("pick2", [P, NT, EXP])
        m1, m2 = sb("m1", [P, NT]), sb("m2", [P, NT])
        f1, f2 = sb("f1", [P, NT]), sb("f2", [P, NT])
        gap, ed = sb("gap", [P, NT]), sb("ed", [P, NT])
        dn, g1, g2 = sb("dn", [P, NT]), sb("g1", [P, NT]), sb("g2", [P, NT])
        wa, wb = sb("wa", [P, NT, EXP]), sb("wb", [P, NT, EXP])
        w_tok = sb("w_tok", [P, NT, EXP])
        wT = sb("wT", [EXP, TOK])
        logitT = wT
        w_bc = sb("w_bc", [P, RING, TOK])

        x_hi = [sb(f"x_hi{i}", [P, TOK], f32r) for i in range(2)]
        x_lo = [sb(f"x_lo{i}", [P, TOK], f32r) for i in range(2)]
        h1 = [sb(f"h1_{i}", [P, 1 + TOK]) for i in range(2)]
        h2 = [sb(f"h2_{i}", [P, 1 + TOK]) for i in range(2)]
        dif = sb("dif", [P, TOK])
        xk, xv, xr = (sb(n, [P, TOK]) for n in ("xk", "xv", "xr"))
        kT, vT = sb("kT", [P, TOK]), sb("vT", [P, TOK])
        rt = kT
        pp, aa, bb = (sb(n, [P, 1 + TOK]) for n in ("pp", "aa", "bb"))
        ex = sb("ex", [P, 4, TOK])
        E1B, E2B, E1, E2 = range(4)
        n2, num, den, rw = (sb(n, [P, TOK]) for n in ("n2", "num", "den", "rw"))
        xk_hi, xv_hi = sb("xk_hi", [P, TOK], f32r), sb("xv_hi", [P, TOK], f32r)
        xk_lo, xv_lo = sb("xk_lo", [P, TOK], f32r), sb("xv_lo", [P, TOK], f32r)
        e2v, th, fin, pm = rw, n2, num, den
        xk2, xr2 = den, rw
        kk = ex
        g_raw = sb("g_raw", [P, HC, TOK])
        g_hi, g_lo = sb("g_hi", [P, 2, HC, TOK], f32r), sb("g_lo", [P, 2, HC, TOK], f32r)
        y_w = sb("y_w", [P, 2, TOK])
        moe = sb("moe", [P, 2, TOK])
        gated = th

        def bank(name):
            return ctx.enter_context(nc.psum_tensor(name, [P, TOK], f32))

        H = [bank(f"ps_h{i}") for i in range(3)]
        Y = bank("ps_y")
        A = [bank(f"ps_a{i}") for i in range(4)]
        FK_BANKS = (2, 3, 1, 2)

        w_dram = nc.dram_tensor("w_scratch", [CHUNKS, EXP, TOK], f32, kind="Internal").ap()
        x_t = x.rearrange("(q n p) c -> q p n c", n=NT, p=P)
        out_t = out.rearrange("(q n p) c -> q p n c", n=NT, p=P)

        S = {name: sem(name) for name in EVENTS}
        vec_in, wr_in, late_in = sem("vec_in"), sem("wr_in"), sem("late_in")
        const_ready, dve_const, negw_ready = sem("const_ready"), sem("dve_const"), sem("negw_ready")
        wr_rounded, wr_split = sem("wr_rounded"), sem("wr_split")

        UNITS = 2 * EXP
        unit_in = [sem(f"unit_in{u}") for u in range(UNITS)]
        roundings, logit_turns = sem("roundings"), sem("logit_turns")
        unit_rounded, unit_split = sem("unit_rounded"), sem("unit_split")
        UNIT_PLACES = (x1_tok[:].rearrange("p n c -> p (n c)"), xs_tok[:].rearrange("p n c -> p (n c)"),
                       h2[0][:, 1:1 + TOK], h2[1][:, 1:1 + TOK])
        ACT_UNITS = range(8, 12)
        kvr_raw = y_w[:, 1, 0:KVR * P].rearrange("p (n c) -> p n c", c=P)
        kvr_in, kvr_rounded, kvr_split = sem("kvr_in"), sem("kvr_rounded"), sem("kvr_split")
        fk_raw = moe[:, 1, :]
        act_unit_rounded, act_unit_split = sem("act_unit_rounded"), sem("act_unit_split")

        def unit_raw(u):
            if u < 4:
                return ex[:, u, :]
            if 8 <= u < 12:
                return (aa[:, 1:1 + TOK], bb[:, 1:1 + TOK], rw[:], num[:])[u % 4]
            return UNIT_PLACES[u % 4]

        def unit_part(u, w1_part, w2_part):
            if u == UNITS - 1:
                return w2_part[:, EXP - 1, :]
            return w1_part[:, (u + 1) // 2, :] if u % 2 or u == 0 else w2_part[:, u // 2 - 1, :]

        def units_until(e):
            return 2 * e if e else 1

        dve_step, pool_step, act_step = sem("dve_step"), sem("pool_step"), sem("act_step")

        def until_hi(eng, b, off, e, j):
            by = SPLIT[e][j][0]
            until(eng, {"A": "act_hi", "P": "pool_hi"}[by], b, off, pair_count(by, None, e, j) + 1)

        def until_lo(eng, b, off, e, j):
            by = SPLIT[e][j][1]
            until(eng, {"V": "dve_lo", "P": "pool_lo"}[by], b, off, pair_count(None, by, e, j) + 1)

        def until(eng, name, b, off, k):
            n = EVENTS[name]
            least = n * off + k
            ahead = n if any(name in names for names in AHEAD.values()) else 0
            if isinstance(b, int):
                if PAIR * n * b + least > 0:
                    eng.wait_ge(S[name], PAIR * n * b + least + ahead)
            else:
                assert least + ahead > 0, (name, off, k)
                eng.wait_ge(S[name], b * (PAIR * n) + (least + ahead))

        def signal_ahead(eng, which):
            for name in AHEAD[which]:
                eng.sem_inc(S[name], EVENTS[name])

        half_step = [0]

        def steps(eng, own):
            count = [0]

            def step(ins):
                count[0] += 1
                ins.then_inc(own, 1)
                return count[0]

            def after(n):
                if n:
                    eng.wait_ge(own, n)

            def restart():
                if count[0]:
                    eng.wait_ge(own, count[0])
                    eng.sem_clear(own)
                    count[0] = 0
                    half_step[0] = 0
            return step, after, restart

        def schedule(eng, slot, restart=None):
            for e in range(CUT):
                slot(0, 0, e)
            if restart:
                restart()
            with eng.Fori(0, CHUNKS // PAIR - 1) as b:
                for off, es in ((0, range(CUT, EXP)), (1, range(EXP)), (2, range(CUT))):
                    for e in es:
                        slot(b, off, e)
                if restart:
                    restart()
            last = CHUNKS // PAIR - 1
            for off, es in ((0, range(CUT, EXP)), (1, range(EXP))):
                for e in es:
                    slot(last, off, e)

        def has(b, off):
            return not isinstance(b, int) or 0 <= PAIR * b + off < CHUNKS

        def bcast(t):
            return t[:].rearrange("p (n o) -> p n o", o=1).to_broadcast([P, NT, EXP])

        block = ctx.enter_context(nc.Block())

        @block.sync
        def _(sp):
            signal_ahead(sp, "sync")
            sp.dma_start(x_tok[0][:], x_t[0]).then_inc(S["x_loaded"], 16)
            sp.dma_start(vec_sb[:], vec).then_inc(vec_in, 16)
            sp.dma_start(wr_sb[:], wr).then_inc(wr_in, 16)

            def load_unit(u):
                sp.dma_start(unit_raw(u), unit_part(u, w1, w2)).then_inc(unit_in[u], 16)

            def spread(q, group):
                first = group * GROUP
                if first >= RING:
                    until(sp, "y_taken", 0, q, first - RING + GROUP)
                else:
                    until(sp, "y_taken", 0, q - 1, EXP + first - RING + GROUP)
                sp.dma_start(w_bc[:, first % RING:first % RING + GROUP, :],
                             w_dram[q:q + 1, first:first + GROUP, :].to_broadcast([P, GROUP, TOK]))\
                  .then_inc(S[f"w_spread{group}"], 16)

            def keep_w(q):
                until(sp, "wT_sb", 0, q, 1)
                sp.dma_start(w_dram[q], wT[:]).then_inc(S["w_stored"], 16)
                until(sp, "w_stored", 0, q, 16)

            def load(q):
                until(sp, "xs_ready", 0, q - 2, 1)
                until(sp, "x_loaded", 0, q - 1, 16)
                sp.dma_start(x_tok[q % 2][:], x_t[q]).then_inc(S["x_loaded"], 16)

            def store(q):
                until(sp, "out_ready", 0, q, 1)
                sp.dma_start(out_t[q], xs_tok[:]).then_inc(S["out_stored"], 16)

            for u in range(2):
                load_unit(u)
            sp.dma_start(b1_sb[:], b1).then_inc(vec_in, 16)
            sp.dma_start(b2_sb[:], b2).then_inc(vec_in, 16)
            for u in range(2, 4):
                load_unit(u)
            load(1)
            for u in range(4, 12):
                load_unit(u)
            keep_w(0)
            spread(0, 0)
            spread(0, 1)
            for u in range(12, UNITS):
                sp.wait_ge(unit_split, u - 8 + 1)
                load_unit(u)
            for q in range(CHUNKS):
                spread(q, 2)
                if q > 0:
                    store(q - 1)
                spread(q, 3)
                if q + 1 < CHUNKS:
                    if q + 2 < CHUNKS:
                        load(q + 2)
                    keep_w(q + 1)
                    spread(q + 1, 0)
                    spread(q + 1, 1)
            store(CHUNKS - 1)
            until(sp, "out_stored", 0, CHUNKS - 1, 16)

        @block.tensor
        def _(pe):
            def split_mm(dst, w_h, w_l, a_h, a_l):
                nc.tensor.matmul(dst, w_h, a_h, start=True, stop=False)
                nc.tensor.matmul(dst, w_h, a_l, start=False, stop=False)
                return nc.tensor.matmul(dst, w_l, a_h, start=False, stop=True)

            def up(b, off, e):
                for m in range(HC):
                    i = HC * e + m
                    if i == 0:
                        until(pe, "xsplit", b, off, 1)
                    if i >= 3:
                        until(pe, "gelu_done", b, off, i - 2)
                    else:
                        until(pe, "gelu_done", b, off - 1, (31, 32, 30)[i])
                    cols = slice(m * P, (m + 1) * P)
                    split_mm(H[i % 3][:], w1_hi[:, e, cols], w1_lo[:, e, cols], x_hi[off % 2][:],
                             x_lo[off % 2][:]).then_inc(S["up_done"], 1)

            def down(b, off, e):
                until(pe, "y_taken", b, off, e)
                for m in range(HC):
                    if m % 2 == 0:
                        until_lo(pe, b, off, e, m // 2)
                    w_h, w_l = (t[:, e, m * P:(m + 1) * P] for t in (w2_hi, w2_lo))
                    nc.tensor.matmul(Y[:], w_h, g_hi[:, e % 2, m, :], start=(m == 0), stop=False)
                    nc.tensor.matmul(Y[:], w_h, g_lo[:, e % 2, m, :], start=False, stop=False)
                    last = nc.tensor.matmul(Y[:], w_l, g_hi[:, e % 2, m, :], start=False, stop=(m == HC - 1))
                last.then_inc(S["y_done"], 1)

            def turn(dst, src, name):
                for n in range(NT):
                    last = nc.tensor.transpose(dst[:, n * P:(n + 1) * P], src(n), ident[:])
                last.then_inc(S[name], 1)

            def front_x(b, off):
                until(pe, "norm_x", b, off, 1)
                until(pe, "relu_done", b, off - 2, HC)
                turn(A[2], lambda n: xn_tok[off % 2][:, n, :], "xnT_ps")

            def front_z(b, off):
                until(pe, "norm1", b, off, 1)
                turn(A[3], lambda n: z_tok[:, n, :], "zT_ps")

            def router(b, off):
                until(pe, "xsplit", b, off, 1)
                until(pe, "out_ready", b, off - 2, 1)
                split_mm(A[1][0:EXP, :], wr_hi[:], wr_lo[:], x_hi[off % 2][:], x_lo[off % 2][:])\
                    .then_inc(S["router_ps"], 1)

            def turn_logits(b, off):
                until(pe, "logitT_sb", b, off, 1)
                pe.sem_inc(logit_turns, 1)
                for n in range(NT):
                    last = nc.tensor.transpose(A[1][:, n * EXP:(n + 1) * EXP], logitT[:, n * P:(n + 1) * P],
                                               ident[0:EXP, 0:EXP])
                last.then_inc(S["logit_ps"], 1)

            def turn_w(b, off):
                until(pe, "w_ready", b, off, 1)
                for n in range(NT):
                    last = nc.tensor.transpose(A[1][0:EXP, n * P:(n + 1) * P], w_tok[:, n, :], ident[:])
                last.then_inc(S["wT_ps"], 1)

            def channel_out(b, off):
                until(pe, *(("v_sb", b, off + 1, 1) if has(b, off + 1) else ("relu_done", b, off, HC - 1)))
                for j in range(HC):
                    until(pe, "kk_ready", b, off, j + 1)
                    last = nc.tensor.matmul(A[1][:], fv_sb[:, j, :], kk[:, j, :], start=(j == 0), stop=(j == HC - 1))
                last.then_inc(S["fv_ps"], 1)

            def finish_turn(b, off):
                until(pe, "fin_ready", b, off, 1)
                turn(A[1], lambda n: fin[:, n * P:(n + 1) * P], "fin_ps")

            def slot(b, off, e):
                first = isinstance(b, int) and PAIR * b + off == 0
                if first:
                    pe.wait_ge(unit_split, units_until(e + 1))
                if e + 1 < EXP:
                    up(b, off, e + 1)
                elif has(b, off + 1):
                    up(b, off + 1, 0)
                if e == 0:
                    if first:
                        pe.wait_ge(kvr_split, 1)
                        pe.wait_ge(late_in, 16 * 3)
                    until(pe, "k_split", b, off, 1)
                    until(pe, "th_ready", b, off - 1, 1)
                    split_mm(A[0][:], kvr_hi[:, 0, :], kvr_lo[:, 0, :], xk_hi[:], xk_lo[:]).then_inc(S["k_ps"], 1)
                    until(pe, "relu_done", b, off - 1, HC - 1)
                    if first:
                        turn_w(b, off)
                        until(pe, "wT_sb", b, off, 1)
                    until(pe, "v_split", b, off, 1)
                    split_mm(A[1][:], kvr_hi[:, 1, :], kvr_lo[:, 1, :], xv_hi[:], xv_lo[:]).then_inc(S["v_ps"], 1)
                if e == 2 and not first:
                    finish_turn(b, off - 1)
                if e == 4 and has(b, off + 1):
                    router(b, off + 1)
                if e == 6:
                    until(pe, "norm2", b, off, 1)
                    until(pe, *(("h1_ready", b, off + 1, 1) if has(b, off + 1)
                                else ("relu_done", b, off - 1, HC)))
                    turn(A[3], lambda n: z2_tok[:, n, :], "h2T_ps")
                if e == 7:
                    if has(b, off + 1):
                        turn_w(b, off + 1)
                    until(pe, "mix2", b, off, 1)
                    until(pe, "x1_ready", b, off, 1)
                    nc.tensor.matmul(A[0][:], proj_sb[:, 1, :], xr2[:], start=True, stop=True).then_inc(S["fr_ps"], 1)
                    until(pe, "xk2_split", b, off, 1)
                    for j in range(HC):
                        if j == 0:
                            until(pe, *(("xsplit", b, off + 1, 1) if has(b, off + 1)
                                        else ("relu_done", b, off - 1, HC)))
                        if j == 1:
                            until(pe, "h2_ready", b, off, 1)
                        if j == 2:
                            until(pe, *(("wT_sb", b, off + 1, 1) if has(b, off + 1)
                                        else ("out_ready", b, off - 1, 1)))
                        if j == 3:
                            until(pe, "relu_done", b, off, 1)
                        cols = slice(j * P, (j + 1) * P)
                        split_mm(A[FK_BANKS[j]][:], fk_hi[:, cols], fk_lo[:, cols], x_hi[off % 2][:], x_lo[off % 2][:])\
                            .then_inc(S["fk_ps"], 1)

                if first:
                    pe.wait_ge(unit_split, units_until(e + 1) + 1)
                down(b, off, e)

                if e == 0 and not first:
                    channel_out(b, off - 1)
                if e == 1:
                    until(pe, "k_sb", b, off, 1)
                    until(pe, "r_split", b, off, 1)
                    split_mm(A[0][:], kvr_hi[:, 2, :], kvr_lo[:, 2, :], x_hi[(off + 1) % 2][:], x_lo[(off + 1) % 2][:])\
                        .then_inc(S["r_ps"], 1)
                    if has(b, off + 1):
                        front_x(b, off + 1)
                        front_z(b, off + 1)
                if e == 4:
                    if has(b, off + 1):
                        turn_logits(b, off + 1)
                    until(pe, "rw_ready", b, off, 1)
                    for n in range(NT):
                        last = nc.tensor.matmul(A[0][:, n * P:(n + 1) * P], rw[:, n * P:(n + 1) * P], proj_sb[:, 0, :],
                                                start=True, stop=True)
                    last.then_inc(S["o_ps"], 1)
                if first and e == CUT - 1:
                    pe.wait_ge(unit_split, UNITS - len(ACT_UNITS))
                    pe.wait_ge(act_unit_split, len(ACT_UNITS) + 1)

            signal_ahead(pe, "tensor")
            pe.wait_ge(const_ready, 2)
            front_x(0, 0)
            pe.wait_ge(wr_split, 1)
            router(0, 0)
            front_z(0, 0)
            turn_logits(0, 0)
            pe.wait_ge(unit_split, units_until(0))
            up(0, 0, 0)
            schedule(pe, slot)
            last = CHUNKS // PAIR - 1
            channel_out(last, 1)
            finish_turn(last, 1)

        @block.scalar
        def _(act):
            act.dma_start(kvr_raw, projs[:, 0:KVR, :]).then_inc(kvr_in, 16)
            act.dma_start(proj_sb[:], projs[:, KVR:, :]).then_inc(late_in, 16)
            act.dma_start(fk_raw, fk).then_inc(late_in, 16)
            act.dma_start(fv_sb[:], fv).then_inc(late_in, 16)

            def gelu(b, off, e):
                def round_pair(j):
                    until(act, "gelu_done", b, off, HC * e + 2 * j + 2)
                    until(act, "y_done", b, off, e - 1)
                    nc.scalar.activation(g_hi[:, e % 2, 2 * j:2 * j + 2, :], g_raw[:, 2 * j:2 * j + 2, :], ACT.Copy)\
                      .then_inc(S["act_hi"], 1)

                for m in range(HC):
                    i = HC * e + m
                    if m % 2 == 0:
                        until_lo(act, b, off if e else off - 1, (e - 1) % EXP, m // 2)
                    until(act, "up_done", b, off, i + 1)
                    nc.scalar.activation(g_raw[:, m, :], H[i % 3][:], ACT.Gelu,
                                         bias=b1_sb[:, e, m:m + 1]).then_inc(S["gelu_done"], 1)
                    if m == 2 and SPLIT[e][0][0] == "A":
                        round_pair(0)
                if SPLIT[e][1][0] == "A":
                    round_pair(1)

            def scaled(b, off, h, src, w_col, b_col, name, freed):
                until(act, freed, b, off - 1, 1)
                if off % 2 == 1:
                    until(act, name, b, off - 1, 1)
                    nc.scalar.activation(h[1][:, 0:1], h[0][:, TOK:TOK + 1], ACT.Copy)
                nc.scalar.activation(h[off % 2][:, 1:1 + TOK], src, ACT.Identity, bias=vec_sb[:, b_col:b_col + 1],
                                     scale=vec_sb[:, w_col:w_col + 1]).then_inc(S[name], 1)

            def front_x(b, off):
                until(act, "xnT_ps", b, off, 1)
                until(act, "r_ps", b, off - 1, 1)
                nc.scalar.activation(x_hi[off % 2][:], A[2][:], ACT.Copy).then_inc(S["x_hi_ready"], 1)

            def front_z(b, off):
                until(act, "zT_ps", b, off, 1)
                scaled(b, off, h1, A[3][:], LN1_W, LN1_B, "h1_ready", "mix1")

            def take_logits(b, off):
                until(act, "router_ps", b, off, 1)
                until(act, "w_stored", b, off - 1, 16)
                nc.scalar.activation(logitT[:], A[1][0:EXP, :], ACT.Copy).then_inc(S["logitT_sb"], 1)

            def take_w(b, off):
                until(act, "wT_ps", b, off, 1)
                nc.scalar.activation(wT[:], A[1][0:EXP, :], ACT.Copy).then_inc(S["wT_sb"], 1)

            def slot(b, off, e):
                if e + 1 < EXP:
                    gelu(b, off, e + 1)
                elif has(b, off + 1):
                    gelu(b, off + 1, 0)
                if e == 0:
                    if isinstance(b, int) and PAIR * b + off == 0:
                        take_w(b, off)
                    until(act, "k_ps", b, off, 1)
                    until(act, "rw_ready", b, off - 1, 1)
                    nc.scalar.activation(kT[:], A[0][:], ACT.Copy).then_inc(S["k_sb"], 1)
                    until(act, "v_ps", b, off, 1)
                    nc.scalar.activation(vT[:], A[1][:], ACT.Copy).then_inc(S["v_sb"], 1)
                if e == 0 and isinstance(b, int) and PAIR * b + off == 0:
                    for u in ACT_UNITS:
                        act.wait_ge(unit_in[u], 16)
                        nc.scalar.activation(unit_part(u, w1_hi, w2_hi), unit_raw(u), ACT.Copy)\
                          .then_inc(act_unit_rounded, 1)
                    act.wait_ge(late_in, 16 * 3)
                    nc.scalar.activation(fk_hi[:], fk_raw, ACT.Copy).then_inc(act_unit_rounded, 1)
                if e == 1:
                    until(act, "args_ready", b, off, 1)
                    nc.scalar.activation(ex[:], ex[:], ACT.Exp).then_inc(S["exp_done"], 1)
                if e == 2:
                    until(act, "r_ps", b, off, 1)
                    until(act, "args_ready", b, off, 1)
                    nc.scalar.activation(rt[:], A[0][:], ACT.Tanh, scale=0.5).then_inc(S["rt_ready"], 1)
                    if has(b, off + 1):
                        front_x(b, off + 1)
                        front_z(b, off + 1)
                if e == 4 and has(b, off + 1):
                    take_logits(b, off + 1)
                if e == 6:
                    until(act, "h2T_ps", b, off, 1)
                    scaled(b, off, h2, A[3][:], LN2_W, LN2_B, "h2_ready", "mix2")
                if e == 7:
                    if has(b, off + 1):
                        take_w(b, off + 1)
                    until(act, "fr_ps", b, off, 1)
                    nc.scalar.activation(th[:], A[0][:], ACT.Tanh, scale=0.5).then_inc(S["th_ready"], 1)
                    until(act, "fv_ps", b, off - 1, 1)
                    for j in range(HC + 1):
                        if j < HC:
                            until(act, "fk_ps", b, off, j + 1)
                            nc.scalar.activation(kk[:, j, :], A[FK_BANKS[j]][:], ACT.Relu)\
                              .then_inc(S["relu_done"], 1)
                        if j > 0:
                            until(act, "relu_done", b, off, j)
                            nc.scalar.activation(kk[:, j - 1, :], kk[:, j - 1, :], ACT.Square)\
                              .then_inc(S["kk_ready"], 1)

            act.wait_ge(vec_in, 16 * 3)
            nc.scalar.activation(negw[:], vec_sb[:, DECAY:DECAY + 1], ACT.Exp).then_inc(act_step, 1)
            act.wait_ge(act_step, 1)
            nc.scalar.activation(negw[:], negw[:], ACT.Copy, scale=-1.0).then_inc(negw_ready, 1)
            act.wait_ge(kvr_in, 16)
            nc.scalar.activation(kvr_hi[:], kvr_raw, ACT.Copy).then_inc(kvr_rounded, 1)
            act.wait_ge(dve_const, 2)
            front_x(0, 0)
            take_logits(0, 0)
            front_z(0, 0)
            gelu(0, 0, 0)
            schedule(act, slot)

        @block.vector
        def _(dve):
            V = nc.vector
            step, after, restart = steps(dve, dve_step)

            def stats(src, bn, mv, ve, name):
                for n in range(NT):
                    t = step(V.bn_stats(bn[:, n, :], src[:, n, :]))
                for n in range(NT):
                    after(t - NT + 1 + n)
                    u = step(V.bn_aggr(mv[:, n, :], bn[:, n, :]))
                after(u)
                V.tensor_scalar(ve[:].rearrange("p (n o) -> p n o", o=1), mv[:, :, 1:2], EPS, None, ALU.add)\
                 .then_inc(S[name], 1)

            def normalize(dst, src, mv, r):
                for n in range(NT):
                    last = V.tensor_scalar(dst[:, n, :], src[:, n, :], mv[:, n, 0:1], r[:, n:n + 1],
                                           ALU.subtract, ALU.mult)
                return last

            def front_stats(b, off):
                until(dve, "x_loaded", b, off, 16)
                stats(x_tok[off % 2], bn1, mv1, ve1, "stat1")

            def norm_x(b, off):
                until(dve, "rstd_x", b, off, 1)
                normalize(xn_tok[off % 2], x_tok[off % 2], mv1, ra).then_inc(S["norm_x"], 1)

            def norm_z(b, off):
                until(dve, "rstd1", b, off, 1)
                until(dve, "h2T_ps", b, off - 2, 1)
                until(dve, "zT_ps", b, off - 1, 1)
                normalize(z_tok, x_tok[off % 2], mv1, rz).then_inc(S["norm1"], 1)

            def split_x(b, off):
                until(dve, "x_hi_ready", b, off, 1)
                V.tensor_tensor(x_lo[off % 2][:], A[2][:], x_hi[off % 2][:].bitcast(f32), ALU.subtract)\
                 .then_inc(S["xsplit"], 1)

            def split_g(b, off, e, j):
                if SPLIT[e][j][1] != "V":
                    return
                until_hi(dve, b, off, e, j)
                part = slice(2 * j, 2 * j + 2)
                V.tensor_tensor(g_lo[:, e % 2, part, :], g_raw[:, part, :], g_hi[:, e % 2, part, :].bitcast(f32),
                                ALU.subtract).then_inc(S["dve_lo"], 1)

            def mixes(h, diff, outs, name):
                now, before = h[:, 1:1 + TOK], h[:, 0:TOK]
                after(step(V.tensor_tensor(diff[:], now, before, ALU.subtract)))
                for dst, mu in outs:
                    last = V.scalar_tensor_tensor(out=dst[:], in0=diff[:], scalar=vec_sb[:, mu:mu + 1], in1=before,
                                                  op0=ALU.mult, op1=ALU.add)
                last.then_inc(S[name], 1)

            def mix1(b, off):
                until(dve, "h1_ready", b, off, 1)
                until(dve, "r_ps", b, off - 1, 1)
                until(dve, "mix2", b, off - 1, 1)
                mixes(h1[off % 2], dif, ((xk, TMK), (xv, TMV), (xr, TMR)), "mix1")

            def first_best(src, peak, same, tie_, f, pick):
                after(step(V.tensor_reduce(out=peak[:], in_=src[:], op=ALU.max, axis=AX.X)))
                after(step(V.tensor_tensor(same[:], src[:], bcast(peak), ALU.is_equal)))
                after(step(V.tensor_tensor(tie_[:], same[:], rank[:].rearrange("p (o e) -> p o e", o=1)
                                           .to_broadcast([P, NT, EXP]), ALU.mult)))
                after(step(V.tensor_reduce(out=f[:], in_=tie_[:], op=ALU.max, axis=AX.X)))
                after(step(V.tensor_tensor(pick[:], tie_[:], bcast(f), ALU.is_equal)))

            def choose(b, off):
                until(dve, "logit_ps", b, off, 1)
                V.tensor_copy(lg[:].rearrange("p n e -> p (n e)"), A[1][:, 0:NT * EXP]).then_inc(S["logit_sb"], 1)
                until(dve, "logit_sb", b, off, 1)
                first_best(lg, m1, eq, tie, f1, pick1)
                after(step(V.scalar_tensor_tensor(out=lg2[:], in0=pick1[:], scalar=MASKED, in1=lg[:],
                                                  op0=ALU.mult, op1=ALU.add)))

            def choose_second(b, off):
                first_best(lg2, m2, eq2, tie2, f2, pick2)
                V.tensor_tensor(gap[:], m2[:], m1[:], ALU.subtract).then_inc(S["ed_arg"], 1)

            def weigh(b, off):
                until(dve, "ed_ready", b, off, 1)
                after(step(V.tensor_scalar(dn[:], ed[:], 1.0, None, ALU.add)))
                after(step(V.reciprocal(g1[:], dn[:])))
                t = step(V.tensor_tensor(g2[:], ed[:], g1[:], ALU.mult))
                u = step(V.tensor_tensor(wa[:], pick1[:], bcast(g1), ALU.mult))
                after(t)
                v = step(V.tensor_tensor(wb[:], pick2[:], bcast(g2), ALU.mult))
                after(v)
                until(dve, "wT_ps", b, off - 1, 1)
                V.tensor_tensor(w_tok[:], wa[:], wb[:], ALU.add).then_inc(S["w_ready"], 1)

            def state_max(b, off):
                until(dve, "k_sb", b, off, 1)
                until(dve, "rw_ready", b, off - 1, 1)
                for t, start in ((pp, NEG_BIG), (aa, 0.0), (bb, 0.0)):
                    s = step(V.tensor_copy(t[:, 0:1], t[:, TOK:TOK + 1]) if off % 2 else V.memset(t[:, 0:1], start))
                after(s)
                half_step[0] = step(V.tensor_tensor_scan(
                    pp[:, 1:1 + TOK], negw[:, 0:1].to_broadcast([P, TOK]), kT[:], pp[:, 0:1], ALU.add, ALU.max))

            def state_args(b, off):
                before, now = pp[:, 0:TOK], pp[:, 1:1 + TOK]
                u = vec_sb[:, FIRST:FIRST + 1]
                until(dve, "fk_ps", b, off - 1, HC)
                after(half_step[0])
                m = step(V.scalar_tensor_tensor(out=pm[:], in0=kT[:], scalar=u, in1=before, op0=ALU.add, op1=ALU.max))
                until(dve, "fv_ps", b, off - 1, 1)
                V.scalar_tensor_tensor(out=ex[:, E1B, :], in0=before, scalar=negw[:, 0:1], in1=now,
                                       op0=ALU.add, op1=ALU.subtract)
                V.tensor_tensor(ex[:, E2B, :], kT[:], now, ALU.subtract)
                after(m)
                V.tensor_tensor(ex[:, E1, :], before, pm[:], ALU.subtract)
                V.scalar_tensor_tensor(out=ex[:, E2, :], in0=kT[:], scalar=u, in1=pm[:],
                                       op0=ALU.add, op1=ALU.subtract).then_inc(S["args_ready"], 1)

            def scan_weights(b, off):
                until(dve, "exp_done", b, off, 1)
                until(dve, "v_sb", b, off, 1)
                until(dve, "fr_ps", b, off - 1, 1)
                V.tensor_tensor_scan(bb[:, 1:1 + TOK], ex[:, E1B, :], ex[:, E2B, :], bb[:, 0:1],
                                     ALU.mult, ALU.add).then_inc(S["bb_ready"], 1)
                half_step[0] = step(V.tensor_tensor(e2v[:], ex[:, E2B, :], vT[:], ALU.mult))

            def scan_values(b, off):
                after(half_step[0])
                after(step(V.tensor_tensor_scan(aa[:, 1:1 + TOK], ex[:, E1B, :], e2v[:], aa[:, 0:1],
                                                ALU.mult, ALU.add)))
                until(dve, "fin_ps", b, off - 1, 1)
                half_step[0] = step(V.tensor_tensor(num[:], ex[:, E1, :], aa[:, 0:TOK], ALU.mult))

            HALVES = (slice(0, TOK // 2), slice(TOK // 2, TOK))

            def receptance(b, off):
                until(dve, "rt_ready", b, off, 1)
                until(dve, "n2_ready", b, off, 1)
                after(half_step[0])
                after(step(V.tensor_tensor(num[:], num[:], n2[:], ALU.add)))
                half_step[0] = step(V.scalar_tensor_tensor(out=num[:], in0=rt[:], scalar=1.0, in1=num[:],
                                                           op0=ALU.add, op1=ALU.mult))

            def receptance_half(b, off):
                until(dve, "den_ready", b, off, 1)
                step(V.reciprocal(den[:, HALVES[0]], den[:, HALVES[0]]))

            def receptance_rest(b, off):
                t = step(V.reciprocal(den[:, HALVES[1]], den[:, HALVES[1]]))
                after(t)
                V.scalar_tensor_tensor(out=rw[:], in0=num[:], scalar=0.5, in1=den[:], op0=ALU.mult, op1=ALU.mult)\
                 .then_inc(S["rw_ready"], 1)

            def take_y(b, off, e):
                if e % GROUP == 0:
                    until(dve, f"w_spread{e // GROUP}", b, off, 16)
                if e == 0:
                    until(dve, "fin_ready", b, off - 2, 1)
                until(dve, "y_done", b, off, e + 1)
                if e == 2:
                    until(dve, "moe_added", b, off - 1, EXP - 1)
                if e >= 3:
                    until(dve, "moe_added", b, off, e - 2)
                dst = moe[:, off % 2, :] if e == 0 else y_w[:, e % 2, :]
                V.scalar_tensor_tensor(out=dst, in0=Y[:], scalar=b2_sb[:, e:e + 1], in1=w_bc[:, e % RING, :],
                                       op0=ALU.add, op1=ALU.mult).then_inc(S["y_taken"], 1)

            def finish_gate(b, off):
                until(dve, "fv_ps", b, off, 1)
                until(dve, "th_ready", b, off, 1)
                after(step(V.scalar_tensor_tensor(out=gated[:], in0=th[:], scalar=1.0, in1=A[1][:],
                                                  op0=ALU.add, op1=ALU.mult)))
                until(dve, "moe_added", b, off, EXP - 1)
                until(dve, "rw_ready", b, off, 1)
                V.scalar_tensor_tensor(out=fin[:], in0=gated[:], scalar=0.5, in1=moe[:, off % 2, :],
                                       op0=ALU.mult, op1=ALU.add).then_inc(S["fin_ready"], 1)

            def finish_out(b, off):
                until(dve, "fin_ps", b, off, 1)
                until(dve, "xs_ready", b, off, 1)
                V.tensor_tensor(xs_tok[:].rearrange("p n c -> p (n c)"), A[1][:],
                                xs_tok[:].rearrange("p n c -> p (n c)"), ALU.add).then_inc(S["out_ready"], 1)

            def x1_stats(b, off):
                until(dve, "o_ps", b, off, 1)
                V.tensor_tensor(x1_tok[:].rearrange("p n c -> p (n c)"), A[0][:],
                                xn_tok[off % 2][:].rearrange("p n c -> p (n c)"), ALU.add).then_inc(S["x1_ready"], 1)
                until(dve, "x1_ready", b, off, 1)
                stats(x1_tok, bn2, mv2, ve2, "stat2")

            def norm2(b, off):
                until(dve, "rstd2", b, off, 1)
                if has(b, off + 1):
                    until(dve, "zT_ps", b, off + 1, 1)
                normalize(z2_tok, x1_tok, mv2, r2).then_inc(S["norm2"], 1)

            def mix2(b, off):
                until(dve, "h2_ready", b, off, 1)
                until(dve, "mix1", b, off, 1)
                now, before = h2[off % 2][:, 1:1 + TOK], h2[off % 2][:, 0:TOK]
                mu_k, mu_r = (vec_sb[:, m:m + 1] for m in (F_TMK, F_TMR))
                after(step(V.tensor_tensor(dif[:], now, before, ALU.subtract)))
                after(step(V.scalar_tensor_tensor(out=xk2[:], in0=dif[:], scalar=mu_k, in1=before,
                                                  op0=ALU.mult, op1=ALU.add)))
                until(dve, "up_done", b, off, EXP * HC)
                hi = step(V.tensor_copy(x_hi[off % 2][:], xk2[:]))
                V.scalar_tensor_tensor(out=xr2[:], in0=dif[:], scalar=mu_r, in1=before,
                                       op0=ALU.mult, op1=ALU.add).then_inc(S["mix2"], 1)
                after(hi)
                V.tensor_tensor(x_lo[off % 2][:], xk2[:], x_hi[off % 2][:].bitcast(f32), ALU.subtract)\
                 .then_inc(S["xk2_split"], 1)

            def slot(b, off, e):
                first = isinstance(b, int) and PAIR * b + off == 0
                ahead = has(b, off + 1)
                nxt = (b, off, e + 1) if e + 1 < EXP else (b, off + 1, 0) if ahead else None

                if first and e == 2:
                    dve.wait_ge(act_unit_split, len(ACT_UNITS))
                if e == 0 and ahead:
                    front_stats(b, off + 1)
                if e == 1:
                    state_args(b, off)
                    if ahead:
                        norm_x(b, off + 1)
                        norm_z(b, off + 1)
                if e == 2:
                    scan_weights(b, off)
                if e == 3:
                    if ahead:
                        split_x(b, off + 1)
                    receptance(b, off)
                if e == 4:
                    receptance_rest(b, off)
                if e == 5:
                    x1_stats(b, off)
                if e == 7 and ahead:
                    mix1(b, off + 1)

                if nxt:
                    split_g(*nxt, 0)
                if e == 1 and not first:
                    finish_gate(b, off - 1)
                if e == 2 and not first:
                    finish_out(b, off - 1)
                if e == 6 and ahead:
                    weigh(b, off + 1)

                if nxt:
                    split_g(*nxt, 1)
                if first:
                    for u in {0: range(4, 8), 1: range(12, UNITS)}.get(e, ()):
                        split_unit(u)
                if e == 0:
                    state_max(b, off)
                if e == 2:
                    scan_values(b, off)
                if e == 3:
                    receptance_half(b, off)
                if e == 4 and ahead:
                    choose(b, off + 1)
                    choose_second(b, off + 1)
                if e == 5:
                    norm2(b, off)
                if e == 6:
                    mix2(b, off)
                take_y(b, off, e)

            def split_unit(u):
                dve.wait_ge(unit_rounded, u + 1 - (len(ACT_UNITS) if u > ACT_UNITS[0] else 0))
                V.tensor_tensor(unit_part(u, w1_lo, w2_lo), unit_raw(u), unit_part(u, w1_hi, w2_hi).bitcast(f32),
                                ALU.subtract).then_inc(unit_split, 1)

            signal_ahead(dve, "vector")
            for t in (h1[0], h2[0]):
                V.memset(t[:, 0:1], 0.0).then_inc(dve_const, 1)
            front_stats(0, 0)
            dve.wait_ge(wr_rounded, 1)
            V.tensor_tensor(wr_lo[:], wr_sb[:], wr_hi[:].bitcast(f32), ALU.subtract).then_inc(wr_split, 1)
            norm_x(0, 0)
            split_unit(0)
            split_x(0, 0)
            norm_z(0, 0)
            split_unit(1)
            dve.wait_ge(kvr_rounded, 1)
            V.tensor_tensor(kvr_lo[:], kvr_raw, kvr_hi[:].bitcast(f32), ALU.subtract).then_inc(kvr_split, 1)
            choose(0, 0)
            choose_second(0, 0)
            mix1(0, 0)
            split_g(0, 0, 0, 0)
            weigh(0, 0)
            split_g(0, 0, 0, 1)
            for u in range(2, 4):
                split_unit(u)
            dve.wait_ge(negw_ready, 1)
            schedule(dve, slot, restart)
            last = CHUNKS // PAIR - 1
            finish_gate(last, 1)
            finish_out(last, 1)

        @block.gpsimd
        def _(pool):
            G = nc.gpsimd
            step, after, restart = steps(pool, pool_step)

            def add_y(b, off, e):
                until(pool, "y_taken", b, off, e + 1)
                if e > 1:
                    until(pool, "moe_added", b, off, e - 1)
                acc = moe[:, off % 2, :]
                G.tensor_tensor(acc, acc, y_w[:, e % 2, :], ALU.add)\
                 .then_inc(S["moe_added"], 1)

            def add_before(b, off, e):
                if e >= 2:
                    add_y(b, off, e - 1)
                elif e == 0 and not (isinstance(b, int) and PAIR * b + off == 0):
                    add_y(b, off - 1, EXP - 1)

            def root_x(b, off):
                until(pool, "stat1", b, off, 1)
                until(pool, "norm1", b, off - 1, 1)
                G.tensor_tensor(ra[:], ve1[:], neg_half[:], ALU.pow).then_inc(S["rstd_x"], 1)

            def root_z(b, off):
                var = mv1[:, :, 1:2].rearrange("p n o -> p (n o)")
                until(pool, "rstd_x", b, off, 1)
                after(step(G.tensor_tensor(rb[:], ra[:], ra[:], ALU.mult)))
                after(step(G.tensor_tensor(rb[:], rb[:], var, ALU.mult)))
                after(step(G.tensor_scalar(rb[:], rb[:], EPS, None, ALU.add)))
                after(step(G.tensor_tensor(rb[:], rb[:], neg_half[:], ALU.pow)))
                G.tensor_tensor(rz[:], ra[:], rb[:], ALU.mult).then_inc(S["rstd1"], 1)

            def round_g(b, off, e, j):
                part = slice(2 * j, 2 * j + 2)
                if SPLIT[e][j][0] == "P":
                    until(pool, "gelu_done", b, off, HC * e + 2 * j + 2)
                    until(pool, "y_done", b, off, e - 1)
                    pool.sem_inc(roundings, 1)
                    G.tensor_scalar(g_hi[:, e % 2, part, :], g_raw[:, part, :], 1.0, 0.0, ALU.mult, ALU.add)\
                     .then_inc(S["pool_hi"], 1)
                if SPLIT[e][j][1] == "P":
                    until_hi(pool, b, off, e, j)
                    G.tensor_tensor(g_lo[:, e % 2, part, :], g_raw[:, part, :], g_hi[:, e % 2, part, :].bitcast(f32),
                                    ALU.subtract).then_inc(S["pool_lo"], 1)

            def split_mix(b, off, raw, hi, lo, name):
                pool.sem_inc(roundings, 1)
                after(step(G.tensor_scalar(hi[:], raw[:], 1.0, 0.0, ALU.mult, ALU.add)))
                G.tensor_tensor(lo[:], raw[:], hi[:].bitcast(f32), ALU.subtract).then_inc(S[name], 1)

            def split_kv(b, off):
                until(pool, "mix1", b, off, 1)
                until(pool, "v_ps", b, off - 1, 1)
                split_mix(b, off, xk, xk_hi, xk_lo, "k_split")
                split_mix(b, off, xv, xv_hi, xv_lo, "v_split")

            def split_r(b, off):
                until(pool, "mix1", b, off, 1)
                until(pool, "fk_ps", b, off - 1, HC)
                split_mix(b, off, xr, x_hi[(off + 1) % 2], x_lo[(off + 1) % 2], "r_split")

            def round_unit(u):
                pool.wait_ge(unit_in[u], 16)
                G.tensor_scalar(unit_part(u, w1_hi, w2_hi), unit_raw(u), 1.0, 0.0, ALU.mult, ALU.add)\
                 .then_inc(unit_rounded, 1)

            def exp_gap(b, off):
                until(pool, "ed_arg", b, off, 1)
                G.tensor_tensor(ed[:], euler[:], gap[:], ALU.pow).then_inc(S["ed_ready"], 1)

            def slot(b, off, e):
                nxt = (b, off, e + 1) if e + 1 < EXP else (b, off + 1, 0) if has(b, off + 1) else None
                if e == 2:
                    until(pool, "exp_done", b, off, 1)
                    until(pool, "v_sb", b, off, 1)
                    until(pool, "fin_ready", b, off - 1, 1)
                    G.tensor_tensor(n2[:], ex[:, E2, :], vT[:], ALU.mult).then_inc(S["n2_ready"], 1)
                if e == 6 and has(b, off + 1):
                    exp_gap(b, off + 1)
                if nxt:
                    round_g(*nxt, 0)
                if e == 3:
                    until(pool, "bb_ready", b, off, 1)
                    after(step(G.tensor_tensor(den[:], ex[:, E1, :], bb[:, 0:TOK], ALU.mult)))
                    G.tensor_tensor(den[:], den[:], ex[:, E2, :], ALU.add).then_inc(S["den_ready"], 1)
                if e == 5:
                    until(pool, "stat2", b, off, 1)
                    G.tensor_tensor(r2[:], ve2[:], neg_half[:], ALU.pow).then_inc(S["rstd2"], 1)
                if e not in ADD_LATE:
                    add_before(b, off, e)
                if nxt:
                    round_g(*nxt, 1)
                if isinstance(b, int) and PAIR * b + off == 0:
                    for u in {0: range(4, 8), 1: range(12, UNITS)}.get(e, ()):
                        round_unit(u)
                if e in ADD_LATE:
                    add_before(b, off, e)
                if e == 0:
                    split_r(b, off)
                if e == 0 and has(b, off + 1):
                    root_x(b, off + 1)
                    root_z(b, off + 1)
                if e < 2 and isinstance(b, int) and PAIR * b + off == 0:
                    for n in (range(0, 2), range(2, len(ACT_UNITS)))[e]:
                        u = ACT_UNITS[n]
                        pool.wait_ge(act_unit_rounded, n + 1)
                        G.tensor_tensor(unit_part(u, w1_lo, w2_lo), unit_raw(u),
                                        unit_part(u, w1_hi, w2_hi).bitcast(f32), ALU.subtract).then_inc(act_unit_split, 1)
                if e == 1 and isinstance(b, int) and PAIR * b + off == 0:
                    pool.wait_ge(act_unit_rounded, len(ACT_UNITS) + 1)
                    G.tensor_tensor(fk_lo[:], fk_raw, fk_hi[:].bitcast(f32), ALU.subtract).then_inc(act_unit_split, 1)
                if e == 7 and has(b, off + 1):
                    split_kv(b, off + 1)
                if e == 6:
                    until(pool, "out_stored", b, off - 1, 16)
                    G.tensor_tensor(xs_tok[:], x_tok[off % 2][:], x1_tok[:], ALU.add).then_inc(S["xs_ready"], 1)

            signal_ahead(pool, "gpsimd")
            step(G.memset(neg_half[:], -0.5))
            step(G.memset(euler[:], float(np.e)))
            step(G.memset(ident[:], 0.0))
            after(step(G.memset(rank[:], 0.0)))
            G.affine_select(out=ident[:], in_=ident[:], compare_op=ALU.not_equal, fill=1.0, base=0,
                            pattern=[[-1, P]], channel_multiplier=1).then_inc(const_ready, 1)
            for e in range(EXP):
                last = G.memset(rank[:, e:e + 1], float(EXP - e))
            last.then_inc(const_ready, 1)
            root_x(0, 0)
            pool.wait_ge(wr_in, 16)
            G.tensor_scalar(wr_hi[:], wr_sb[:], 1.0, 0.0, ALU.mult, ALU.add).then_inc(wr_rounded, 1)
            round_unit(0)
            root_z(0, 0)
            for u in range(1, 4):
                round_unit(u)
            exp_gap(0, 0)
            round_g(0, 0, 0, 0)
            round_g(0, 0, 0, 1)
            split_kv(0, 0)
            schedule(pool, slot, restart)
            add_y(CHUNKS // PAIR - 1, 1, EXP - 1)


def kernel(L0_attn_x, L0_attn_ln1_w, L0_attn_ln1_b, L0_attn_ln2_w, L0_attn_ln2_b, L0_attn_time_decay,
           L0_attn_time_first, L0_attn_tmk, L0_attn_tmv, L0_attn_tmr, L0_attn_att_kw, L0_attn_att_vw,
           L0_attn_att_rw, L0_attn_att_ow, L0_attn_f_tmk, L0_attn_f_tmr, L0_attn_f_kw, L0_attn_f_rw,
           L0_attn_f_vw, L0_ffn_Wr, L0_ffn_W1, L0_ffn_b1, L0_ffn_W2, L0_ffn_b2):
    import concourse.bacc as bacc
    from concourse.bass_utils import run_bass_kernel_spmd

    def lay(a):
        return np.ascontiguousarray(a)

    a = np.asarray
    arrays = dict(
        x=lay(a(L0_attn_x).reshape(BATCH * TIME, CH)),
        vec=lay(np.stack([a(v) for v in (
            L0_attn_ln1_w, L0_attn_ln1_b, L0_attn_ln2_w, L0_attn_ln2_b, L0_attn_time_decay, L0_attn_time_first,
            L0_attn_tmk, L0_attn_tmv, L0_attn_tmr, L0_attn_f_tmk, L0_attn_f_tmr)], axis=1)),
        projs=lay(np.stack([a(w).T for w in (
            L0_attn_att_kw, L0_attn_att_vw, L0_attn_att_rw, L0_attn_att_ow, L0_attn_f_rw)], axis=1)),
        fk=lay(a(L0_attn_f_kw).T),
        fv=lay(a(L0_attn_f_vw).T.reshape(HC, P, CH).transpose(1, 0, 2)),
        wr=lay(a(L0_ffn_Wr).T),
        w1=lay(a(L0_ffn_W1).transpose(2, 0, 1)),
        b1=lay(a(L0_ffn_b1).reshape(EXP, HC, P).transpose(2, 0, 1)),
        w2=lay(a(L0_ffn_W2).transpose(0, 2, 1).reshape(EXP, HC, P, CH).transpose(2, 0, 1, 3).reshape(P, EXP, HID)),
        b2=lay(a(L0_ffn_b2).T),
    )
    nc = bacc.Bacc("TRN2", target_bir_lowering=False, num_devices=1)
    args = [nc.dram_tensor(n, v.shape, mybir.dt.from_np(v.dtype), kind="ExternalInput").ap() for n, v in arrays.items()]
    out = nc.dram_tensor("out", (BATCH * TIME, CH), mybir.dt.float32, kind="ExternalOutput").ap()
    build(nc, *args, out)
    r = run_bass_kernel_spmd(nc, [arrays], core_ids=[0])
    return r.results[0]["out"].reshape(BATCH, TIME, CH)
```
